# Optimizing a Trainium2 kernel written in Bass

```python
import numpy as np
import jax
import jax.numpy as jnp

def _softmax(x, axis=-1):
    return jax.nn.softmax(x, axis=axis)

def _gelu(x):
    return jax.nn.gelu(x, approximate=True)

def _silu(x):
    return jax.nn.silu(x)

def _sigmoid(x):
    return jax.nn.sigmoid(x)

def _layernorm(x, axis=-1, eps=1e-05):
    m = jnp.mean(x, axis=axis, keepdims=True)
    v = jnp.var(x, axis=axis, keepdims=True)
    return (x - m) / jnp.sqrt(v + eps)

def _scatter_add(tgt, idx, src, axis=0):
    return tgt.at[idx].add(src)

def _segment_sum(src, seg, n):
    return jax.ops.segment_sum(src, seg, n)
kernel_name = 'mk_seq_postln_d1_jaxref_r8_c8509b'

def setup_inputs(seed: int=0):
    np.random.seed(seed)
    _w = jnp.asarray

    def _L0_attn_setup():
        import jax, jax.numpy as jnp
        import numpy as np
        B, T, D, H = (2, 256, 128, 16)
        HD = D // H
        key = jax.random.key(seed)
        ks = jax.random.split(key, 9)
        w = lambda k, shp: jax.random.normal(k, shp, jnp.float32) * 0.02
        return {'x': jax.random.normal(ks[0], (B, T, D), jnp.float32), 'Wq': w(ks[1], (D, D)), 'bq': jnp.zeros((D,), jnp.float32), 'Wk': w(ks[2], (D, D)), 'bk': jnp.zeros((D,), jnp.float32), 'Wv': w(ks[3], (D, D)), 'bv': jnp.zeros((D,), jnp.float32), 'Wo': w(ks[4], (D, D)), 'bo': jnp.zeros((D,), jnp.float32), 'Wqs': w(ks[5], (3, HD)), 'bqs': jnp.zeros((3,), jnp.float32), 'Wks': w(ks[6], (3, HD)), 'bks': jnp.zeros((3,), jnp.float32), 'Wvs': w(ks[7], (3, HD)), 'bvs': jnp.zeros((3,), jnp.float32), 'temp': jnp.float32(1.0)}
    _L0_attn_in = _L0_attn_setup()

    def _L0_ffn_setup():
        import jax, jax.numpy as jnp
        import numpy as np
        HIDDEN = 128
        INTER = 512
        key = jax.random.key(seed)
        k1, k2, k3, k4, k5 = jax.random.split(key, 5)
        hidden_states = jax.random.normal(k1, (4, 256, HIDDEN), dtype=jnp.float32)
        W1 = jax.random.normal(k2, (HIDDEN, INTER), dtype=jnp.float32) * (1.0 / np.sqrt(HIDDEN))
        b1 = jax.random.normal(k3, (INTER,), dtype=jnp.float32) * 0.02
        W2 = jax.random.normal(k4, (INTER, HIDDEN), dtype=jnp.float32) * (1.0 / np.sqrt(INTER))
        b2 = jax.random.normal(k5, (HIDDEN,), dtype=jnp.float32) * 0.02
        return {'hidden_states': hidden_states, 'W1': W1, 'b1': b1, 'W2': W2, 'b2': b2}
    _L0_ffn_in = _L0_ffn_setup()
    _d = {'L0_attn_x': _L0_attn_in['x'], 'L0_attn_Wq': _L0_attn_in['Wq'], 'L0_attn_bq': _L0_attn_in['bq'], 'L0_attn_Wk': _L0_attn_in['Wk'], 'L0_attn_bk': _L0_attn_in['bk'], 'L0_attn_Wv': _L0_attn_in['Wv'], 'L0_attn_bv': _L0_attn_in['bv'], 'L0_attn_Wo': _L0_attn_in['Wo'], 'L0_attn_bo': _L0_attn_in['bo'], 'L0_attn_Wqs': _L0_attn_in['Wqs'], 'L0_attn_bqs': _L0_attn_in['bqs'], 'L0_attn_Wks': _L0_attn_in['Wks'], 'L0_attn_bks': _L0_attn_in['bks'], 'L0_attn_Wvs': _L0_attn_in['Wvs'], 'L0_attn_bvs': _L0_attn_in['bvs'], 'L0_attn_temp': _L0_attn_in['temp'], 'L0_ffn_W1': _L0_ffn_in['W1'], 'L0_ffn_b1': _L0_ffn_in['b1'], 'L0_ffn_W2': _L0_ffn_in['W2'], 'L0_ffn_b2': _L0_ffn_in['b2']}
    _x0 = _d['L0_attn_x']
    _d['L0_attn_x'] = jax.random.normal(jax.random.fold_in(jax.random.key(seed), 1), (4, 1024, 128), dtype=_x0.dtype)
    del _x0
    return _d

def reference(L0_attn_x, L0_attn_Wq, L0_attn_bq, L0_attn_Wk, L0_attn_bk, L0_attn_Wv, L0_attn_bv, L0_attn_Wo, L0_attn_bo, L0_attn_Wqs, L0_attn_bqs, L0_attn_Wks, L0_attn_bks, L0_attn_Wvs, L0_attn_bvs, L0_attn_temp, L0_ffn_W1, L0_ffn_b1, L0_ffn_W2, L0_ffn_b2):

    def _L0_attn_ref(x, Wq, bq, Wk, bk, Wv, bv, Wo, bo, Wqs, bqs, Wks, bks, Wvs, bvs, temp):
        import jax, jax.numpy as jnp
        import numpy as np
        B, T, D, H = (2, 256, 128, 16)
        HD = D // H
        Bx, Tx, Dx = x.shape
        split = lambda y: y.reshape(Bx, Tx, H, HD).transpose(0, 2, 1, 3)
        q = split(x @ Wq.T + bq)
        k = split(x @ Wk.T + bk)
        v = split(x @ Wv.T + bv)
        q_stp = q @ Wqs.T + bqs
        k3 = k @ Wks.T + bks
        v3 = v @ Wvs.T + bvs
        cross_kv = jnp.cross(k3, v3, axis=-1)
        scores = (jnp.einsum('bhqd,bhkd->bhqk', q, k) + jnp.einsum('bhqc,bhkc->bhqk', q_stp, cross_kv)) * temp
        attn = jax.nn.softmax(scores, axis=-1)
        out = jnp.einsum('bhqk,bhkd->bhqd', attn, v)
        out = out.transpose(0, 2, 1, 3).reshape(Bx, Tx, Dx)
        return out @ Wo.T + bo

    def _L0_ffn_ref(hidden_states, W1, b1, W2, b2):
        import jax, jax.numpy as jnp
        import numpy as np
        HIDDEN = 128
        INTER = 512
        h = jax.nn.relu(jnp.einsum('bsh,hi->bsi', hidden_states, W1) + b1)
        return jnp.einsum('bsi,ih->bsh', h, W2) + b2
    x = L0_attn_x
    x = _layernorm(x + _L0_attn_ref(x, L0_attn_Wq, L0_attn_bq, L0_attn_Wk, L0_attn_bk, L0_attn_Wv, L0_attn_bv, L0_attn_Wo, L0_attn_bo, L0_attn_Wqs, L0_attn_bqs, L0_attn_Wks, L0_attn_bks, L0_attn_Wvs, L0_attn_bvs, L0_attn_temp), axis=-1)
    x = _layernorm(x + _L0_ffn_ref(x, L0_ffn_W1, L0_ffn_b1, L0_ffn_W2, L0_ffn_b2), axis=-1)
    return x

_drawn_inputs = setup_inputs


def setup_inputs(seed=0):
    import zlib

    import numpy as np

    out = dict(_drawn_inputs(seed))
    spreads = {'L0_attn_bq': (0.0, 0.8),
     'L0_attn_bk': (0.0, 0.8),
     'L0_attn_bv': (0.0, 0.387),
     'L0_attn_bo': (0.0, 0.1),
     'L0_attn_bqs': (0.0, 0.8),
     'L0_attn_bks': (0.0, 0.8),
     'L0_attn_bvs': (0.0, 0.8)}
    factors = {'L0_attn_Wq': 8.0,
     'L0_attn_Wk': 8.0,
     'L0_attn_Wv': 8.0,
     'L0_attn_Wqs': 8.0,
     'L0_attn_Wks': 8.0,
     'L0_attn_Wvs': 8.0,
     'L0_ffn_b1': 5.084,
     'L0_ffn_b2': 3.42}
    for name, (base, spread) in spreads.items():
        noise = np.random.default_rng([zlib.crc32(name.encode()), seed]).standard_normal(out[name].shape)
        drawn = base * np.exp(spread * noise) if base else spread * noise
        out[name] = jnp.asarray(drawn.astype(out[name].dtype))
    for name, factor in factors.items():
        out[name] = (out[name] * factor).astype(out[name].dtype)
    return out
```

```python
from contextlib import ExitStack

import numpy as np
import concourse.bass as bass
from concourse import mybir

F32 = mybir.dt.float32
BF16 = mybir.dt.bfloat16
ACT = mybir.ActivationFunctionType
ALU = mybir.AluOpType
AX_X = mybir.AxisListType.X

BATCH, TOK, D, H = 4, 1024, 128, 16
HD = D // H
INTER = 512
P = 128
HALF = TOK // 2
TILES = TOK // P
HT = HALF // P
GROUPS = 4
GH = H // GROUPS
UNITS = 2 * GROUPS
FC = INTER // P
KM = 6 * HD
KB = KM + 3
KS = KB + 3
C3 = 3 * H
CR = 64 + C3
VW = 32
EPS = 1e-5
SCORE_RING, ROW_RING = 3, 2

_W = {}
_at = 0
for _name, _width in (
    ("ident", P), ("wqT", P), ("wkT", P), ("wk", P), ("wv", P), ("selAC", CR), ("selBD", CR), ("cols", 16),
    ("wvT", P), ("wqs", P), ("bqs", H), ("bv_row", P), ("woT", P), ("bo_row", P), ("b2_row", P),
    ("w1", INTER), ("w2", INTER)):
    _W[_name] = (_at, _width)
    _at += _width
W_COLS = _at
W_FIRST = _W["wvT"][0]
COL = {"bq": 0, "bk": 1, "bv": 2, "bksAC": 3, "bvsBD": 4, "temp": 5, "sign": 6, "b1": 7}

COUNTS = {
    "weights": {"score": 1},
    "x_load": {"x": 16},
    "xT": {"score": 1},
    "ac": {"score": 1},
    "bd": {"row": 1},
    "q": {"score": 1},
    "k": {"score": 1},
    "kbias": {"score": 1},
    "v": {"row": 1},
    "split": {"split": 1, "pool_step": 3},
    "store": {"stored": 16},
    "load": {},
    "stage_v": {"staged": 1},
    "max_split": {"max_split": 1, "dve_step": 3},
    "max_rows": {"row": 1, "max_stored": 16},
    "resid": {"resid": 16, "resid_bo": 1},
    "norm": {"row": 1, "dve_step": 1},
    "oT": {"score": 1},
    "wo": {"row": 1, "dve_step": 1, "ln_stats": 1, "pool_step": 2, "ln1": 1, "x1_b2": 1},
    "x1T": {"score": 1},
    "ffn1": {"score": 1},
    "ffn2": {"row": 1, "dve_step": 1, "ln_stats": 1, "pool_step": 2, "out": 1, "out_stored": 16},
}
NAMES = ("score", "row", "pv", "saved", "x", "split", "stored", "loaded0", "loaded1", "loaded2", "loaded3", "staged",
         "max_split", "max_stored", "shift0", "shift1", "resid", "resid_bo", "ln_stats", "ln1", "x1_b2", "out", "out_stored",
         "dve_step", "pool_step")
LOAD_DMAS, SHIFT_DMAS, N_STORES = 6, 2, 7


def counts_of(job):
    kind, i = job[0], job[1]
    if kind == "store":
        return {"stored": 16 * (3 if i < 2 else 1)}
    if kind == "load":
        return {f"loaded{i}": 16 * LOAD_DMAS}
    if kind == "max_rows":
        return COUNTS[kind] | {f"shift{i % 2}": 16 * SHIFT_DMAS}
    return COUNTS[kind]


def tail_jobs(half):
    jobs = {(0, 1): [("resid", half)], (1, 0): [("oT", half)], (1, 2): [("wo", half)], (1, 6): [("x1T", half)],
            (2, 5): [("ffn2", half)]}
    for t in range(HT):
        jobs[(0, 2 + t)] = [("norm", (half, t))]
    for c in range(FC):
        jobs[(2, c)] = [("ffn1", (half, c))]
    return jobs


PROJECT = {(0, 0): [("x_load", 0)], (0, 6): [("xT", 0)], (0, 7): [("xT", 1)], (1, 1): [("q", 0)], (1, 3): [("q", 1)],
           (1, 4): [("split", 0), ("ac", 0)], (1, 5): [("ac", 1)], (1, 7): [("bd", 0)], (2, 4): [("bd", 1)],
           (2, 6): [("k", 0)], (2, 7): [("k", 1)], (3, 0): [("split", 1), ("store", 0), ("kbias", 0)],
           (3, 2): [("kbias", 1)], (3, 3): [("split", 2)], (3, 4): [("v", 0)], (4, 1): [("store", 1), ("store", 2)]}
PROJECT_FIRST = [("xT", 0), ("xT", 1), ("q", 0), ("ac", 0), ("q", 1), ("split", 0), ("ac", 1), ("bd", 0), ("bd", 1),
                 ("k", 0), ("k", 1), ("split", 1), ("kbias", 0), ("kbias", 1), ("split", 2), ("v", 0),
                 ("store", 0), ("store", 1), ("store", 2), ("load", 0), ("load", 1), ("load", 2), ("load", 3),
                 ("stage_v", 0), ("stage_v", 1), ("stage_v", 2), ("stage_v", 3)]


class Step:
    def __init__(self, exp=None, maxima=(), pv=None, finished=None, jobs=()):
        self.exp, self.maxima, self.pv, self.finished, self.jobs = exp, list(maxima), pv, finished, list(jobs)


def max_tiles(unit, s):
    return [(unit, n // GH, n % GH) for n in (2 * s, 2 * s + 1)]


def batch_steps(project_next, tail_before):
    steps = []
    for u in range(UNITS):
        for s in range(TILES):
            jobs = []
            if s == 0 and (u + 1 < UNITS or project_next):
                jobs.append(("max_split", u + 1))
            if s == 1 and (u + 1 < UNITS or project_next):
                jobs.append(("max_rows", u + 1))
            if tail_before:
                jobs += tail_jobs(1).get((u, s), [])
            jobs += tail_jobs(0).get((u - GROUPS, s), [])
            if project_next:
                jobs += PROJECT.get((u, s), [])
                if u > GROUPS and s == 1:
                    jobs += [("load", u - GROUPS - 1), ("stage_v", u - GROUPS - 1)]
            maxima = max_tiles(u + 2, s) if u + 2 < UNITS or project_next else []
            pv = (u, s - 1) if s else ((u - 1, TILES - 1) if u else None)
            steps.append(Step((u, s), maxima, pv, u - 1 if s == 0 and u else None, jobs))
    last = [("load", GROUPS - 1), ("stage_v", GROUPS - 1)] if project_next else []
    steps.append(Step(None, [], (UNITS - 1, TILES - 1), UNITS - 1, last))
    return steps


def opening_steps():
    steps = [Step(jobs=[("weights", 0), ("x_load", 0)] + PROJECT_FIRST)]
    steps += [Step(maxima=max_tiles(0, s)) for s in range(TILES)]
    steps += [Step(maxima=max_tiles(1, s), jobs=[[("max_split", 0)], [("max_rows", 0)]][s] if s < 2 else [])
              for s in range(TILES)]
    return steps


def closing_steps():
    return [Step(jobs=j) for _, j in sorted(tail_jobs(1).items())]


class Segment:

    def __init__(self, steps):
        self.steps = steps
        self.total = dict.fromkeys(NAMES, 0)
        self.number = {}
        for n, step in enumerate(steps):
            if step.exp:
                for hh in range(GH):
                    self._count("score", ("exp", step.exp, hh))
            for tile in step.maxima:
                self._count("row", ("max", tile))
            if step.pv:
                self._count("pv", step.pv)
            if step.finished is not None:
                self._count("saved", step.finished)
            for job in step.jobs:
                for name, by in counts_of(job).items():
                    self._count(name, job, by)

    def _count(self, name, key, by=1):
        self.total[name] += by
        self.number[name, key] = self.total[name]

    def after(self, name, key):
        return self.base[name] + self.number.get((name, key), 0)


def build(nc, x, w, out):
    opening = Segment(opening_steps())
    first = Segment(batch_steps(True, False))
    middle = Segment(batch_steps(True, True))
    last = Segment(batch_steps(False, True))
    closing = Segment(closing_steps())
    loops = BATCH - 2

    def start_of(segment, i=0):
        before = {opening: [], first: [opening], middle: [opening, first], last: [opening, first] + [middle] * loops,
                  closing: [opening, first] + [middle] * loops + [last]}[segment]
        base = {n: sum(s.total[n] for s in before) for n in NAMES}
        if segment is middle:
            base = {n: i * middle.total[n] + base[n] if middle.total[n] else base[n] for n in NAMES}
        segment.base = base
        segment.opening = segment is opening
        segment.batch = {opening: -1, first: 0, middle: i + 1, last: BATCH - 1, closing: BATCH}[segment]

    def program(eng, emit):
        for segment in (opening, first):
            start_of(segment)
            emit(segment)
        with eng.Fori(0, loops) as i:
            start_of(middle, i)
            emit(middle)
        for segment in (last, closing):
            start_of(segment)
            emit(segment)

    def wait(eng, sem, count):
        if not isinstance(count, int) or count > 0:
            eng.wait_ge(sem, count)

    def alone(eng):
        eng.nop(nofuse=True)

    with ExitStack() as ctx:
        def sb(name, shape, dt):
            return ctx.enter_context(nc.sbuf_tensor(name, shape, dt))

        wt = sb("wt", [P, W_COLS], F32)
        ident_b = sb("ident_b", [P, P], BF16)
        w_ac = sb("w_ac", [P, 2 * CR], F32)
        b_ac = sb("b_ac", [P, 2], F32)
        wqs_s = sb("wqs_s", [P, P], F32)
        bqs_s = sb("bqs_s", [P, H], F32)
        bq_t = sb("bq_t", [P, 1], F32)
        x_in = sb("x_in", [P, TILES, D], F32)
        xT = sb("xT", [P, TOK], F32)
        k3v = sb("k3v", [P, TOK], F32)
        cross = sb("cross", [P, TOK], F32)
        val = [sb("q_val", [P, TOK], F32), sb("k_val", [P, TOK], F32), sb("kb_val", [P, TOK], F32)]
        parts = [sb("q_parts", [P, 3, TOK], BF16), sb("k_parts", [P, 3, TOK], BF16), sb("kb_parts", [P, 3, TOK], BF16)]
        rest = sb("rest", [P, TOK], F32)
        v_next = sb("v_next", [P, TILES, D], F32)
        v_cur = sb("v_cur", [P, TILES, H, VW], F32)
        q_op = sb("q_op", [P, H // 2, TOK], BF16)
        k_op = sb("k_op", [P, H // 2, TOK], BF16)
        probs = sb("probs", [P, 2, GH, HALF], F32)
        neg_max = sb("neg_max", [P, 2, GH, HT], F32)
        max_parts = sb("max_parts", [P, GH, 3, HT], BF16)
        max_rest = sb("max_rest", [P, 2, GH, HT], F32)
        max_row = sb("max_row", [GH * 3 * HT, P], BF16)
        attn = sb("attn", [P, 2, GROUPS, HALF], F32)
        recip = sb("recip", [P, HT, H], F32)
        o_tok = sb("o_tok", [P, HT, D], F32)
        oT = sb("oT", [P, HALF], F32)
        resid_in = sb("resid_in", [P, HT, D], F32)
        resid_bo = sb("resid_bo", [P, HT, D], F32)
        pre_ln = sb("pre_ln", [P, HT, D], F32)
        stats = sb("stats", [P, HT, 6], F32)
        mean_var = sb("mean_var", [P, HT, 2], F32)
        rstd = sb("rstd", [P, HT], F32)
        minus_half = sb("minus_half", [P, HT], F32)
        x1 = sb("x1", [P, HT, D], F32)
        x1_b2 = sb("x1_b2", [P, HT, D], F32)
        x1T = sb("x1T", [P, HALF], F32)
        hid = sb("hid", [P, FC, HALF], F32)
        y = sb("y", [P, HT, D], F32)

        row_bank = [ctx.enter_context(nc.psum_tensor(f"row_bank{i}", [P, TOK], F32)) for i in range(ROW_RING)]
        score_bank = [ctx.enter_context(nc.psum_tensor(f"score_bank{i}", [P, HALF], F32)) for i in range(SCORE_RING)]
        pv_bank = ctx.enter_context(nc.psum_tensor("pv_bank", [P, HALF], F32))

        stacked = [nc.dram_tensor(f"stacked_{n}", (P, 6, TOK), BF16, kind="Internal").ap() for n in "qk"]
        stacked_kb = nc.dram_tensor("stacked_kb", (H, 3, TOK), BF16, kind="Internal").ap()
        stacked_max = nc.dram_tensor("stacked_max", (2, GH * 3 * HT, P), BF16, kind="Internal").ap()

        S = {n: ctx.enter_context(nc.semaphore(n)) for n in
             ("w_first", "w_rest", "cleared", "prepared", "score_filled", "score_read", "row_filled", "row_read",
              "pv_done", "attn_saved", "x_loaded", "parts_split", "parts_stored", "group0_loaded", "group1_loaded",
              "group2_loaded", "group3_loaded", "values_staged", "max_split", "max_stored", "shift0_loaded",
              "shift1_loaded", "resid_loaded", "resid_biased", "ln_stats", "ln1_done", "x1_biased", "out_ready", "out_stored",
              "dve_step", "pool_step")}
        group_loaded = [S[f"group{g}_loaded"] for g in range(GROUPS)]
        shift_loaded = [S["shift0_loaded"], S["shift1_loaded"]]

        def W(name, a=0, n=None, rows=slice(0, P)):
            at, width = _W[name]
            return wt[rows, at + a:at + (width if n is None else a + n)]

        def col(name, i=0, rows=slice(0, P)):
            return W("cols", COL[name] + i, 1, rows)

        def half_of(t, h):
            return t[:, h * HALF:(h + 1) * HALF]

        def by_tile(bank):
            return bank.rearrange("p (t d) -> p t d", d=D)

        def head_rows(hh):
            return 64 * (hh % 2), hh // 2

        block = ctx.enter_context(nc.Block())

        @block.tensor
        def _(pe):
            def emit(seg):
                def score_slot(key):
                    n = seg.number["score", key] - 1
                    wait(pe, S["score_read"], seg.base["score"] + max(n - SCORE_RING + 1, 0))
                    return score_bank[n % SCORE_RING]

                def row_slot(key):
                    n = seg.number["row", key] - 1
                    wait(pe, S["row_read"], seg.base["row"] + max(n - ROW_RING + 1, 0))
                    return row_bank[n % ROW_RING]

                def scores(u, c, hh):
                    r, pair = head_rows(hh)
                    qh, g = divmod(u, GROUPS)
                    bank = score_slot(("exp", (u, c), hh))
                    rows = slice(r, r + KS)
                    nc.tensor.matmul(bank[:], k_op[rows, 2 * g + pair, c * P:(c + 1) * P],
                                     q_op[rows, 2 * g + pair, qh * HALF:(qh + 1) * HALF],
                                     start=True, stop=True).then_inc(S["score_filled"], 1)

                def max_pass(tiles):
                    for tile in tiles:
                        unit, t, hh = tile
                        r, pair = head_rows(hh)
                        qh, g = divmod(unit % UNITS, GROUPS)
                        if t == 0 and hh == 0:
                            wait(pe, group_loaded[g], seg.after(f"loaded{g}", ("load", g)) if unit >= UNITS
                                 or unit < 2 else seg.base[f"loaded{g}"])
                        bank = row_slot(("max", tile))
                        q0 = qh * HALF + t * P
                        for kh in range(2):
                            mm = nc.tensor.matmul(half_of(bank, kh), q_op[r:r + KB, 2 * g + pair, q0:q0 + P],
                                                  half_of(k_op[r:r + KB, 2 * g + pair], kh), start=True, stop=True)
                            if kh:
                                mm.then_inc(S["row_filled"], 1)
                            yield

                def values(u, c):
                    g = u % GROUPS
                    wait(pe, S["score_read"], seg.after("score", ("exp", (u, c), GH - 1)))
                    if c == 0:
                        wait(pe, S["attn_saved"], seg.base["saved"] + u)
                        if u < GROUPS:
                            wait(pe, S["values_staged"], seg.base["staged"])
                    for hh in range(GH):
                        mm = nc.tensor.matmul(pv_bank[VW * hh:VW * (hh + 1), :], v_cur[:, c, GH * g + hh, :],
                                              probs[:, c % 2, hh, :], start=(c == 0), stop=(c == TILES - 1))
                    mm.then_inc(S["pv_done"], 1)

                def job(kind, i):
                    if kind == "weights":
                        pe.wait_ge(S["w_first"], 16)
                        bank = score_slot((kind, i))
                        for n, (a, s, b) in enumerate((("wk", "selAC", "bk"), ("wv", "selBD", "bv"))):
                            nc.tensor.matmul(bank[:, n * CR:(n + 1) * CR], W(a), W(s), start=True, stop=True)
                            mm = nc.tensor.matmul(bank[0:CR, 2 * CR + n:2 * CR + n + 1], W(s), col(b),
                                                  start=True, stop=True)
                        mm.then_inc(S["score_filled"], 1)
                    elif kind == "xT":
                        wait(pe, S["x_loaded"], seg.after("x", ("x_load", 0)))
                        bank = score_slot((kind, i))
                        for t in range(HT):
                            mm = nc.tensor.transpose(bank[:, t * P:(t + 1) * P], x_in[:, HT * i + t, :], W("ident"))
                        mm.then_inc(S["score_filled"], 1)
                    elif kind in ("q", "ac"):
                        wait(pe, S["score_read"], seg.after("score", ("xT", i)))
                        if kind == "ac" and seg.opening:
                            pe.wait_ge(S["score_read"], seg.after("score", ("weights", 0)))
                        bank = score_slot((kind, i))
                        lhs, rows = (W("wqT"), P) if kind == "q" else (w_ac[:, 0:CR], CR)
                        nc.tensor.matmul(bank[0:rows, :], lhs, half_of(xT, i), start=True,
                                         stop=True).then_inc(S["score_filled"], 1)
                    elif kind == "bd":
                        bank = row_slot((kind, i))
                        nc.tensor.matmul(bank[0:CR, 0:HALF], w_ac[:, CR:2 * CR], half_of(xT, i), start=True,
                                         stop=True).then_inc(S["row_filled"], 1)
                    elif kind == "k":
                        wait(pe, S["row_read"], seg.after("row", ("bd", i)))
                        if seg.opening and i == 0:
                            pe.wait_ge(S["prepared"], 5)
                        bank = score_slot((kind, i))
                        nc.tensor.matmul(bank[:], W("wkT"), half_of(xT, i), start=True, stop=False)
                        nc.tensor.matmul(bank[:], wqs_s[0:CR, :], half_of(cross[0:CR], i), start=False,
                                         stop=True).then_inc(S["score_filled"], 1)
                    elif kind == "kbias":
                        bank = score_slot((kind, i))
                        nc.tensor.matmul(bank[0:H, :], bqs_s[0:CR, :], half_of(cross[0:CR], i), start=True,
                                         stop=True).then_inc(S["score_filled"], 1)
                    elif kind == "v":
                        if seg.opening:
                            pe.wait_ge(S["w_rest"], 16)
                        bank = by_tile(row_slot((kind, i))[:])
                        for t in range(TILES):
                            mm = nc.tensor.matmul(bank[:, t, :], xT[:, t * P:(t + 1) * P], W("wvT"),
                                                  start=True, stop=True)
                        mm.then_inc(S["row_filled"], 1)
                    elif kind == "max_rows":
                        wait(pe, S["max_split"], seg.after("max_split", ("max_split", i)))
                        bank = row_slot((kind, i))[:].bitcast(BF16)
                        alone(pe)
                        nc.tensor.transpose(bank[0:GH * 3 * HT, 0:P], max_parts[:].rearrange("p h r t -> p (h r t)"),
                                            ident_b[:]).then_inc(S["row_filled"], 1)
                    elif kind == "norm":
                        half, t = i
                        wait(pe, S["attn_saved"], seg.after("saved", GROUPS - 1) if half == 0 else seg.base["saved"])
                        bank = by_tile(row_slot((kind, i))[:])
                        for g in range(GROUPS):
                            mm = nc.tensor.transpose(bank[:, g, :], attn[:, half, g, t * P:(t + 1) * P], W("ident"))
                        mm.then_inc(S["row_filled"], 1)
                    elif kind == "oT":
                        wait(pe, S["row_read"], seg.after("row", ("norm", (i, HT - 1))))
                        bank = score_slot((kind, i))
                        for t in range(HT):
                            mm = nc.tensor.transpose(bank[:, t * P:(t + 1) * P], o_tok[:, t, :], W("ident"))
                        mm.then_inc(S["score_filled"], 1)
                    elif kind == "wo":
                        wait(pe, S["score_read"], seg.after("score", ("oT", i)))
                        bank = by_tile(row_slot((kind, i))[:])
                        for t in range(HT):
                            mm = nc.tensor.matmul(bank[:, t, :], oT[:, t * P:(t + 1) * P], W("woT"),
                                                  start=True, stop=True)
                        mm.then_inc(S["row_filled"], 1)
                    elif kind == "x1T":
                        wait(pe, S["ln1_done"], seg.after("ln1", ("wo", i)))
                        bank = score_slot((kind, i))
                        for t in range(HT):
                            mm = nc.tensor.transpose(bank[:, t * P:(t + 1) * P], x1[:, t, :], W("ident"))
                        mm.then_inc(S["score_filled"], 1)
                    elif kind == "ffn1":
                        half, c = i
                        wait(pe, S["score_read"], seg.after("score", ("x1T", half)))
                        bank = score_slot((kind, i))
                        nc.tensor.matmul(bank[:], W("w1", c * P, P), x1T[:], start=True,
                                         stop=True).then_inc(S["score_filled"], 1)
                    elif kind == "ffn2":
                        wait(pe, S["score_read"], seg.after("score", ("ffn1", (i, FC - 1))))
                        bank = by_tile(row_slot((kind, i))[:])
                        for t in range(HT):
                            for c in range(FC):
                                mm = nc.tensor.matmul(bank[:, t, :], hid[:, c, t * P:(t + 1) * P], W("w2", c * P, P),
                                                      start=(c == 0), stop=(c == FC - 1))
                        mm.then_inc(S["row_filled"], 1)

                for step in seg.steps:
                    rows = max_pass(step.maxima)
                    if step.exp:
                        u, c = step.exp
                        if c == 0:
                            key = ("max_rows", u)
                            wait(pe, shift_loaded[u % 2], seg.after(f"shift{u % 2}", key))
                        for hh in range(GH):
                            scores(u, c, hh)
                            next(rows, None)
                    for _ in rows:
                        pass
                    if step.pv:
                        values(*step.pv)
                    for kind, i in step.jobs:
                        job(kind, i)

            pe.wait_ge(S["cleared"], 4)
            program(pe, emit)

        @block.scalar
        def _(act):
            def emit(seg):
                def filled(key):
                    n = seg.number["score", key] - 1
                    wait(act, S["score_filled"], seg.base["score"] + n + 1)
                    return score_bank[n % SCORE_RING]

                def job(kind, i):
                    if kind == "weights":
                        bank = filled((kind, i))
                        nc.scalar.activation(w_ac[:], bank[:, 0:2 * CR], ACT.Identity)
                        nc.scalar.activation(b_ac[0:CR, 0:1], bank[0:CR, 2 * CR:2 * CR + 1], ACT.Identity,
                                             bias=col("bksAC", rows=slice(0, CR)))
                        nc.scalar.activation(b_ac[0:CR, 1:2], bank[0:CR, 2 * CR + 1:2 * CR + 2], ACT.Identity,
                                             bias=col("bvsBD", rows=slice(0, CR))).then_inc(S["score_read"], 1)
                    elif kind == "xT":
                        bank = filled((kind, i))
                        nc.scalar.activation(half_of(xT, i), bank[:], ACT.Identity).then_inc(S["score_read"], 1)
                    elif kind == "ac":
                        bank = filled((kind, i))
                        if seg.opening and i == 0:
                            act.wait_ge(S["score_read"], seg.after("score", ("weights", 0)))
                        nc.scalar.activation(half_of(k3v[0:CR], i), bank[0:CR, :], ACT.Identity,
                                             bias=b_ac[0:CR, 0:1]).then_inc(S["score_read"], 1)
                    elif kind in ("q", "k", "kbias"):
                        bank = filled((kind, i))
                        which = ("q", "k", "kbias").index(kind)
                        if i == 0:
                            wait(act, S["parts_split"], seg.base["split"])
                        if kind == "q":
                            if seg.opening and i == 0:
                                act.wait_ge(S["prepared"], 1)
                            nc.scalar.activation(half_of(val[0], i), bank[:], ACT.Identity, scale=col("temp"),
                                                 bias=bq_t[:]).then_inc(S["score_read"], 1)
                        elif kind == "k":
                            nc.scalar.activation(half_of(val[1], i), bank[:], ACT.Identity,
                                                 bias=col("bk")).then_inc(S["score_read"], 1)
                        else:
                            nc.scalar.activation(half_of(val[2][0:H], i), bank[0:H, :],
                                                 ACT.Identity).then_inc(S["score_read"], 1)
                    elif kind == "oT":
                        bank = filled((kind, i))
                        nc.scalar.activation(oT[:], bank[:], ACT.Identity).then_inc(S["score_read"], 1)
                    elif kind == "x1T":
                        bank = filled((kind, i))
                        nc.scalar.activation(x1T[:], bank[:], ACT.Identity).then_inc(S["score_read"], 1)
                    elif kind == "ffn1":
                        bank = filled((kind, i))
                        nc.scalar.activation(hid[:, i[1], :], bank[:], ACT.Relu,
                                             bias=col("b1", i[1])).then_inc(S["score_read"], 1)

                for step in seg.steps:
                    if step.exp:
                        u, c = step.exp
                        wait(act, S["pv_done"], seg.base["pv"] + max(TILES * u + c - 1, 0))
                        for hh in range(GH):
                            bank = filled(("exp", (u, c), hh))
                            nc.scalar.activation(probs[:, c % 2, hh, :], bank[:], ACT.Exp).then_inc(S["score_read"], 1)
                    if step.finished is not None:
                        wait(act, S["pv_done"], seg.after("pv", step.pv))
                        qh, g = divmod(step.finished, GROUPS)
                        nc.scalar.activation(attn[:, qh, g, :], pv_bank[:], ACT.Identity).then_inc(S["attn_saved"], 1)
                    for kind, i in step.jobs:
                        job(kind, i)

            act.wait_ge(S["w_first"], 16)
            program(act, emit)

        @block.vector
        def _(dve):
            done = [0]

            def emit(seg):
                done[0] = 0

                def then(ins):
                    done[0] += 1
                    ins.then_inc(S["dve_step"], 1)
                    dve.wait_ge(S["dve_step"], seg.base["dve_step"] + done[0])

                def filled(key):
                    n = seg.number["row", key] - 1
                    wait(dve, S["row_filled"], seg.base["row"] + n + 1)
                    return row_bank[n % ROW_RING]

                def statistics():
                    for t in range(HT):
                        last = nc.vector.bn_stats(stats[:, t, :], pre_ln[:, t, :])
                    then(last)
                    alone(dve)
                    for t in range(HT):
                        last = nc.vector.bn_aggr(mean_var[:, t, :], stats[:, t, :])
                    last.then_inc(S["ln_stats"], 1)

                def job(kind, i):
                    if kind == "bd":
                        bank = filled((kind, i))
                        dve.wait_ge(S["score_read"], seg.after("score", ("ac", i)))
                        nc.vector.scalar_tensor_tensor(out=half_of(cross[0:CR], i), in0=bank[0:CR, 0:HALF],
                                                       scalar=b_ac[0:CR, 1:2], in1=half_of(k3v[0:CR], i),
                                                       op0=ALU.add, op1=ALU.mult).then_inc(S["row_read"], 1)
                    elif kind == "v":
                        bank = filled((kind, i))
                        wait(dve, S["values_staged"], seg.base["staged"])
                        bv = W("bv_row").unsqueeze(1).broadcast_to([P, TILES, D])
                        nc.vector.tensor_tensor(v_next[:], by_tile(bank[:]), bv, ALU.add).then_inc(S["row_read"], 1)
                    elif kind == "max_split":
                        buf = i % 2
                        tile = ("max", (i, HT - 1, GH - 1))
                        dve.wait_ge(S["row_read"], seg.after("row", tile))
                        nm, r = neg_max[:, buf], max_rest
                        then(nc.vector.tensor_copy(max_parts[:, :, 0, :], nm))
                        then(nc.vector.tensor_tensor(r[:, 0], nm, max_parts[:, :, 0, :], ALU.subtract))
                        then(nc.vector.tensor_copy(max_parts[:, :, 1, :], r[:, 0]))
                        nc.vector.tensor_tensor(max_parts[:, :, 2, :], r[:, 0], max_parts[:, :, 1, :],
                                                ALU.subtract).then_inc(S["max_split"], 1)
                    elif kind == "max_rows":
                        bank = filled((kind, i))
                        wait(dve, S["max_stored"], seg.after("max_stored", (kind, i)) - 16)
                        nc.vector.tensor_copy(max_row[:], bank[:].bitcast(BF16)[0:GH * 3 * HT, 0:P])\
                            .then_inc(S["row_read"], 1)
                    elif kind == "norm":
                        bank = filled((kind, i))
                        heads = bank[:, 0:GROUPS * P].rearrange("p (h r) -> p h r", r=VW)
                        then(nc.vector.reciprocal(recip[:, i[1], :], heads[:, :, HD]))
                        nc.vector.tensor_tensor(o_tok[:, i[1], :].rearrange("p (h d) -> p h d", d=HD),
                                                heads[:, :, 0:HD], recip[:, i[1], :].unsqueeze(2).broadcast_to([P, H, HD]),
                                                ALU.mult).then_inc(S["row_read"], 1)
                    elif kind == "wo":
                        bank = filled((kind, i))
                        wait(dve, S["resid_biased"], seg.after("resid_bo", ("resid", i)))
                        half = ("ffn2", i)
                        wait(dve, S["out_ready"], seg.after("out", half) - 1)
                        b = by_tile(bank[:, 0:HALF])
                        nc.vector.tensor_tensor(pre_ln[:], b, resid_bo[:], ALU.add).then_inc(S["row_read"], 1)
                        dve.wait_ge(S["row_read"], seg.after("row", (kind, i)))
                        statistics()
                    elif kind == "ffn2":
                        bank = filled((kind, i))
                        wait(dve, S["x1_biased"], seg.after("x1_b2", ("wo", i)))
                        b = by_tile(bank[:, 0:HALF])
                        nc.vector.tensor_tensor(pre_ln[:], b, x1_b2[:], ALU.add).then_inc(S["row_read"], 1)
                        dve.wait_ge(S["row_read"], seg.after("row", (kind, i)))
                        statistics()

                for step in seg.steps:
                    for tile in step.maxima:
                        unit, t, hh = tile
                        bank = filled(("max", tile))
                        nc.vector.tensor_reduce(neg_max[:, unit % 2, hh, t:t + 1], bank[:], AX_X, ALU.max,
                                                negate=True).then_inc(S["row_read"], 1)
                    for kind, i in step.jobs:
                        job(kind, i)
                    
            nc.vector.memset(q_op[:].rearrange("p a t -> p (a t)"), 1.0).then_inc(S["cleared"], 1)
            nc.vector.memset(k_op[:].rearrange("p a t -> p (a t)"), 1.0).then_inc(S["cleared"], 1)
            dve.wait_ge(S["w_first"], 16)
            nc.vector.tensor_scalar(bq_t[:], col("bq"), col("temp"), None, ALU.mult).then_inc(S["prepared"], 1)
            nc.vector.tensor_copy(ident_b[:], W("ident")).then_inc(S["prepared"], 1)
            dve.wait_ge(S["w_rest"], 16)
            nc.vector.tensor_scalar(wqs_s[0:CR], W("wqs", rows=slice(0, CR)), col("sign", rows=slice(0, CR)), None,
                                    ALU.mult).then_inc(S["prepared"], 1)
            nc.vector.tensor_scalar(bqs_s[0:CR], W("bqs", rows=slice(0, CR)), col("sign", rows=slice(0, CR)),
                                    col("temp", rows=slice(0, CR)), ALU.mult, ALU.mult).then_inc(S["prepared"], 1)
            nc.vector.memset(minus_half[:], -0.5).then_inc(S["prepared"], 1)
            program(dve, emit)

        @block.gpsimd
        def _(pool):
            def emit(seg):
                done = [0]

                def then(ins):
                    done[0] += 1
                    ins.then_inc(S["pool_step"], 1)
                    pool.wait_ge(S["pool_step"], seg.base["pool_step"] + done[0])
                    alone(pool)

                def normalise(to, key):
                    pool.wait_ge(S["ln_stats"], seg.after("ln_stats", key))
                    alone(pool)
                    then(nc.gpsimd.tensor_scalar(rstd[:], mean_var[:, :, 1], EPS, None, ALU.add))
                    then(nc.gpsimd.tensor_tensor(rstd[:], rstd[:], minus_half[:], ALU.pow))
                    for t in range(HT):
                        last = nc.gpsimd.tensor_scalar(to[:, t, :], pre_ln[:, t, :], mean_var[:, t, 0:1],
                                                       rstd[:, t:t + 1], ALU.subtract, ALU.mult)
                    return last

                def job(kind, i):
                    if kind == "split":
                        rows = H if i == 2 else P
                        v, part, r = val[i][0:rows, :], parts[i], rest[0:rows, :]
                        pool.wait_ge(S["score_read"], seg.after("score", (("q", "k", "kbias")[i], 1)))
                        wait(pool, S["parts_stored"], seg.base["stored"])
                        alone(pool)
                        then(nc.gpsimd.tensor_copy(part[0:rows, 0, :], v))
                        then(nc.gpsimd.tensor_tensor(r, v, part[0:rows, 0, :], ALU.subtract))
                        then(nc.gpsimd.tensor_copy(part[0:rows, 1, :], r))
                        nc.gpsimd.tensor_tensor(part[0:rows, 2, :], r, part[0:rows, 1, :],
                                                ALU.subtract).then_inc(S["parts_split"], 1)
                    elif kind == "stage_v":
                        pool.wait_ge(S["row_read"], seg.after("row", ("v", 0)))
                        if not seg.opening:
                            pool.wait_ge(S["pv_done"], seg.after("pv", (GROUPS + i, TILES - 1)))
                        alone(pool)
                        heads = slice(GH * i, GH * (i + 1))
                        nc.gpsimd.tensor_copy(v_cur[:, :, heads, 0:HD],
                                              v_next[:].rearrange("p t (h d) -> p t h d", d=HD)[:, :, heads, :])\
                            .then_inc(S["values_staged"], 1)
                    elif kind == "resid":
                        wait(pool, S["resid_loaded"], seg.after("resid", (kind, i)))
                        wait(pool, S["ln1_done"], seg.after("ln1", ("wo", i)) - 1)
                        nc.gpsimd.tensor_tensor(resid_bo[:], resid_in[:],
                                                W("bo_row").unsqueeze(1).broadcast_to([P, HT, D]),
                                                ALU.add).then_inc(S["resid_biased"], 1)
                    elif kind == "wo":
                        normalise(x1, (kind, i)).then_inc(S["ln1_done"], 1)
                        pool.wait_ge(S["ln1_done"], seg.after("ln1", (kind, i)))
                        nc.gpsimd.tensor_tensor(x1_b2[:], x1[:], W("b2_row").unsqueeze(1).broadcast_to([P, HT, D]),
                                                ALU.add).then_inc(S["x1_biased"], 1)
                    elif kind == "ffn2":
                        wait(pool, S["out_stored"], seg.after("out_stored", (kind, i)) - 16)
                        normalise(y, (kind, i)).then_inc(S["out_ready"], 1)

                for step in seg.steps:
                    for kind, i in step.jobs:
                        job(kind, i)

            nc.gpsimd.memset(v_cur[:].rearrange("p c h w -> p (c h w)"), 0.0).then_inc(S["cleared"], 1)
            pool.wait_ge(S["cleared"], 3)
            nc.gpsimd.memset(v_cur[:].rearrange("p c h w -> p (c h) w")[:, :, HD:HD + 1], 1.0).then_inc(S["cleared"], 1)
            pool.wait_ge(S["w_rest"], 16)
            pool.wait_ge(S["cleared"], 4)
            pool.wait_ge(S["prepared"], 5)
            program(pool, emit)

        @block.sync
        def _(sp):
            def batch_rows(t, b, half=None):
                rows = t[bass.ds(b, 1)].rearrange("b (t p) d -> p (b t) d", p=P)
                return rows if half is None else rows[:, half * HT:(half + 1) * HT, :]

            def emit(seg):
                def job(kind, i):
                    if kind == "x_load":
                        wait(sp, S["score_filled"], seg.base["score"])
                        alone(sp)
                        if seg.opening:
                            return
                        sp.dma_start(x_in[:], batch_rows(x, seg.batch + 1)).then_inc(S["x_loaded"], 16)
                    elif kind == "store":
                        sp.wait_ge(S["parts_split"], seg.after("split", ("split", i)))
                        alone(sp)
                        if i == 0:
                            for g in range(GROUPS):
                                wait(sp, group_loaded[g], seg.base[f"loaded{g}"])
                                alone(sp)
                        part = parts[i]
                        if i == 0:
                            for n, slots in ((0, slice(0, 3)), (1, slice(3, 5)), (2, slice(5, 6))):
                                width = slots.stop - slots.start
                                sp.dma_start(stacked[0][:, slots, :],
                                             part[:, n, :].unsqueeze(1).broadcast_to([P, width, TOK]))\
                                    .then_inc(S["parts_stored"], 16)
                        elif i == 1:
                            for slots, n in ((slice(0, 3), 3), (slice(3, 5), 2), (slice(5, 6), 1)):
                                sp.dma_start(stacked[1][:, slots, :], part[:, 0:n, :])\
                                    .then_inc(S["parts_stored"], 16)
                        else:
                            sp.dma_start(stacked_kb[:], part[0:H]).then_inc(S["parts_stored"], 16)
                    elif kind == "load":
                        sp.wait_ge(S["parts_stored"], seg.after("stored", ("store", 2)))
                        alone(sp)
                        if seg.opening:
                            sp.wait_ge(S["cleared"], 2)
                        else:
                            sp.wait_ge(S["pv_done"], seg.after("pv", (GROUPS + i, TILES - 1)))
                        for j in range(2):
                            heads = slice(GH * i + j, GH * (i + 1), 2)
                            pairs = slice(2 * i, 2 * i + 2)
                            for op, src in ((q_op, stacked[0]), (k_op, stacked[1])):
                                by_head = src.rearrange("(h d) s t -> h (d s) t", d=HD)
                                sp.dma_start(op[64 * j:64 * j + KM, pairs, :],
                                             by_head[heads].rearrange("h r t -> r h t"))\
                                    .then_inc(group_loaded[i], 16)
                            sp.dma_start(k_op[64 * j + KM:64 * j + KB, pairs, :],
                                         stacked_kb[heads].rearrange("h r t -> r h t")).then_inc(group_loaded[i], 16)
                    elif kind == "max_rows":
                        sp.wait_ge(S["row_read"], seg.after("row", (kind, i)))
                        sp.dma_start(stacked_max[i % 2], max_row[:]).then_inc(S["max_stored"], 16)
                        sp.wait_ge(S["max_stored"], seg.after("max_stored", (kind, i)))
                        qh, g = divmod(i % UNITS, GROUPS)
                        by_row = stacked_max[i % 2].rearrange("(a j r t) q -> a j r (t q)", a=2, j=2, r=3)
                        for j in range(2):
                            sp.dma_start(q_op[64 * j + KB:64 * j + KS, 2 * g:2 * g + 2, qh * HALF:(qh + 1) * HALF],
                                         by_row[:, j].rearrange("a r q -> r a q")).then_inc(shift_loaded[i % 2], 16)
                    elif kind == "resid":
                        wait(sp, S["resid_biased"], seg.after("resid_bo", (kind, i)) - 1)
                        alone(sp)
                        b = seg.batch - 1 if i == 1 else seg.batch
                        sp.dma_start(resid_in[:], batch_rows(x, b, i)).then_inc(S["resid_loaded"], 16)
                    elif kind == "ffn2":
                        sp.wait_ge(S["out_ready"], seg.after("out", (kind, i)))
                        alone(sp)
                        b = seg.batch - 1 if i == 1 else seg.batch
                        sp.dma_start(batch_rows(out, b, i), y[:]).then_inc(S["out_stored"], 16)

                for step in seg.steps:
                    for kind, i in step.jobs:
                        job(kind, i)

            sp.dma_start(wt[:, 0:W_FIRST], w[:, 0:W_FIRST]).then_inc(S["w_first"], 16)
            sp.dma_start(x_in[:], batch_rows(x, 0)).then_inc(S["x_loaded"], 16)
            sp.dma_start(wt[:, W_FIRST:], w[:, W_FIRST:]).then_inc(S["w_rest"], 16)
            program(sp, emit)
            sp.wait_ge(S["out_stored"], closing.after("out_stored", ("ffn2", 1)))


def pack(i):
    f = np.float32
    Wks, Wvs, Wqs = (np.asarray(i["L0_attn_" + n], f) for n in ("Wks", "Wvs", "Wqs"))
    bks, bvs, bqs = (np.asarray(i["L0_attn_" + n], f) for n in ("bks", "bvs", "bqs"))
    get = lambda n: np.asarray(i["L0_attn_" + n], f)
    w = np.zeros((P, W_COLS), f)

    def put(name, a, at=0):
        a = np.atleast_2d(a)
        w[0:a.shape[0], _W[name][0] + at:_W[name][0] + at + a.shape[1]] = a

    put("ident", np.eye(P, dtype=f))
    put("wqT", get("Wq").T), put("wkT", get("Wk").T), put("wvT", get("Wv").T), put("woT", get("Wo").T)
    put("wk", get("Wk")), put("wv", get("Wv"))
    for h in range(H):
        for c in range(3):
            for at, kc, vc in ((0, (c + 1) % 3, (c + 2) % 3), (64, (c + 2) % 3, (c + 1) % 3)):
                r = at + 3 * h + c
                w[HD * h:HD * (h + 1), _W["selAC"][0] + r] = Wks[kc]
                w[HD * h:HD * (h + 1), _W["selBD"][0] + r] = Wvs[vc]
                w[r, _W["cols"][0] + COL["bksAC"]] = bks[kc]
                w[r, _W["cols"][0] + COL["bvsBD"]] = bvs[vc]
                w[r, _W["wqs"][0] + HD * h:_W["wqs"][0] + HD * (h + 1)] = Wqs[c]
                w[r, _W["bqs"][0] + h] = bqs[c]
    for name in ("bq", "bk", "bv"):
        put("cols", get(name)[:, None], COL[name])
    put("cols", np.full((P, 1), get("temp"), f), COL["temp"])
    put("cols", np.where(np.arange(P) < 64, 1, -1).astype(f)[:, None], COL["sign"])
    put("cols", np.asarray(i["L0_ffn_b1"], f).reshape(FC, P).T, COL["b1"])
    for name, b in (("bv_row", get("bv")), ("bo_row", get("bo")), ("b2_row", np.asarray(i["L0_ffn_b2"], f))):
        put(name, np.broadcast_to(b, (P, D)))
    put("w1", np.asarray(i["L0_ffn_W1"], f))
    put("w2", np.asarray(i["L0_ffn_W2"], f).reshape(FC, P, D).transpose(1, 0, 2).reshape(P, FC * D))
    return w


def kernel(**inputs):
    import concourse.bacc as bacc
    from concourse.bass_utils import run_bass_kernel_spmd

    nc = bacc.Bacc("TRN2", target_bir_lowering=False, num_devices=1)
    arrays = {"x": np.ascontiguousarray(inputs["L0_attn_x"]), "weights": pack(inputs)}
    x, w = (nc.dram_tensor(n, a.shape, F32, kind="ExternalInput").ap() for n, a in arrays.items())
    out = nc.dram_tensor("out", (BATCH, TOK, D), F32, kind="ExternalOutput").ap()
    build(nc, x, w, out)
    return run_bass_kernel_spmd(nc, [arrays], core_ids=[0]).results[0]["out"]
```

```python
from contextlib import ExitStack

import numpy as np
import concourse.bass as bass
from concourse import mybir

F32 = mybir.dt.float32
BF16 = mybir.dt.bfloat16
ACT = mybir.ActivationFunctionType
ALU = mybir.AluOpType
AX_X = mybir.AxisListType.X

BATCH, TOK, D, H = 4, 1024, 128, 16
HD = D // H
INTER = 512
P = 128
HALF = TOK // 2
TILES = TOK // P
HT = HALF // P
GROUPS = 4
GH = H // GROUPS
UNITS = 2 * GROUPS
FC = INTER // P
KM = 6 * HD
KB = KM + 3
KS = KB + 3
WARMING = 16
C3 = 3 * H
CR = 64 + C3
VW = 32
EPS = 1e-5
TWO_ONES = float(np.array([0x3F803F80], np.uint32).view(np.float32)[0])
SCORE_RING, ROW_RING = 3, 2

_W = {}
_at = 0
for _name, _width in (
    ("ident", P), ("wqT", P), ("wkT", P), ("wk", P), ("wv", P), ("selAC", CR), ("selBD", CR), ("cols", 16),
    ("wvT", P), ("wqs", P), ("bqs", H), ("bv_row", P), ("woT", P), ("bo_row", P), ("b2_row", P),
    ("w1", INTER), ("w2", INTER)):
    _W[_name] = (_at, _width)
    _at += _width
W_COLS = _at
W_FIRST = _W["wvT"][0]
COL = {"bq": 0, "bk": 1, "bv": 2, "bksAC": 3, "bvsBD": 4, "temp": 5, "sign": 6, "b1": 7}

COUNTS = {
    "weights": {"score": 1},
    "x_load": {"x": 16},
    "xT": {"score": 1},
    "ac": {"score": 1},
    "bd": {"row": 1},
    "q": {"score": 1},
    "k": {"score": 1},
    "kbias": {"score": 1},
    "v": {"row": 1},
    "split": {"split": 1, "pool_step": 3},
    "split_first": {"split": 1, "dve_step": 3},
    "store_kb": {"kb_stored": 16},
    "stage_v": {"staged": 1},
    "max_split": {"max_split": 1, "dve_step": 3},
    "max_rows": {"row": 1, "max_stored": 16},
    "resid": {"resid": 16, "resid_bo": 1},
    "norm": {"row": 1, "dve_step": 1},
    "warm": {},
    "oT": {"score": 1},
    "wo": {"row": 1},
    "stats1": {"dve_step": 1, "ln_stats": 1, "pool_step": 2, "ln1": 1, "x1_b2": 1},
    "x1T": {"score": 1},
    "ffn1": {"score": 1},
    "ffn2": {"row": 1},
    "stats2": {"dve_step": 1, "ln_stats": 1, "pool_step": 2, "out": 1, "out_stored": 16},
}
NAMES = ("score", "row", "pv", "saved", "x", "split", "stored0", "stored1", "stored2", "stored3", "kb_stored", "loaded0", "loaded1", "loaded2", "loaded3",
         "staged", "max_split", "max_stored", "shift0", "shift1", "resid", "resid_bo", "ln_stats", "ln1", "x1_b2", "out",
         "out_stored", "dve_step", "pool_step")
LOAD_DMAS, LOAD_KB_DMAS, SHIFT_DMAS, STORE_DMAS = 4, 2, 2, 6
LEAD = 12


def counts_of(job):
    kind, i = job[0], job[1]
    if kind == "store":
        return {f"stored{i}": 16 * STORE_DMAS}
    if kind == "load":
        return {f"loaded{i % GROUPS}": 16 * LOAD_DMAS}
    if kind == "load_kb":
        return {f"loaded{i % GROUPS}": 16 * LOAD_KB_DMAS}
    if kind == "max_rows":
        return COUNTS[kind] | {f"shift{i % 2}": 16 * SHIFT_DMAS}
    return COUNTS[kind]


def tail_jobs(half):
    jobs = {(0, 0): [("resid", half)], (0, 6): [("oT", half)], (0, 7): [("wo", half)], (1, 0): [("stats1", half)],
            (1, 3): [("x1T", half)], (3, 0): [("ffn2", half)], (3, 1): [("stats2", half)]}
    for t in range(HT):
        jobs[(0, t)] = jobs.get((0, t), []) + [("norm", (half, t))]
    for c, at in enumerate(((1, 4), (1, 5), (2, 4), (2, 5))):
        jobs[at] = [("ffn1", (half, c))]
    return jobs


PROJECT = {(0, 0): [("x_load", 0)], (0, 4): [("xT", 0)], (0, 5): [("xT", 1)], (1, 1): [("q", 0)], (1, 2): [("q", 1)],
           (1, 3): [("split", 0)], (1, 6): [("ac", 0)], (1, 7): [("bd", 0)], (2, 1): [("ac", 1)], (2, 2): [("bd", 1)],
           (2, 3): [("k", 0)], (2, 6): [("k", 1)], (2, 7): [("split", 1), ("kbias", 0)], (3, 4): [("kbias", 1)],
           (3, 5): [("split", 2)], (3, 6): [("v", 0)],
           (4, 6): [("store", 0), ("store_kb", 0)], (4, 7): [("store", 1)], (5, 2): [("store", 2)], (5, 3): [("store", 3)]}
PROJECT_FIRST = [("xT", 0), ("xT", 1), ("q", 0), ("q", 1), ("split_first", (0, None)), ("ac", 0), ("ac", 1), ("bd", 0),
                 ("bd", 1), ("k", 0), ("k", 1), ("kbias", 0), ("kbias", 1), ("split_first", (1, 0)),
                 ("split_first", (1, 1)), ("split_first", (2, None)), ("store", 0), ("store_kb", 0), ("load", 0),
                 ("load_kb", 0), ("store", 1), ("load", 1), ("load_kb", 1), ("store", 2), ("load", 2), ("load_kb", 2),
                 ("store", 3), ("load", 3), ("load_kb", 3), ("v", 0), ("stage_v", 0), ("stage_v", 1), ("stage_v", 2),
                 ("stage_v", 3)]


class Step:
    def __init__(self, exp=None, maxima=(), pv=None, finished=None, jobs=()):
        self.exp, self.maxima, self.pv, self.finished, self.jobs = exp, list(maxima), pv, finished, list(jobs)


def max_tiles(step):
    return [(step // TILES, n // GH, n % GH) for n in (2 * (step % TILES), 2 * (step % TILES) + 1)]


def batch_steps(project_next, tail_before):
    steps = []
    for u in range(UNITS):
        for s in range(TILES):
            jobs = []
            if s == 4 and (u + 1 < UNITS or project_next):
                jobs.append(("max_split", u + 1))
            if s == 5 and (u + 1 < UNITS or project_next):
                jobs.append(("max_rows", u + 1))
            if tail_before and (u, s) == (0, 1):
                jobs += [("load", -1), ("load_kb", -1), ("stage_v", -1)]
            if tail_before:
                jobs += tail_jobs(1).get((u, s), [])
            jobs += tail_jobs(0).get((u - GROUPS, s), [])
            if project_next:
                jobs += PROJECT.get((u, s), [])
                if u > GROUPS and s == 1:
                    jobs += [("load", u - GROUPS - 1), ("load_kb", u - GROUPS - 1), ("stage_v", u - GROUPS - 1)]
            ahead = u * TILES + s + LEAD
            maxima = max_tiles(ahead) if ahead < UNITS * TILES or project_next else []
            any_before = tail_before or (u, s) != (0, 0)
            pv = divmod(u * TILES + s - 1, TILES) if any_before else None
            steps.append(Step((u, s), maxima, pv, u - 1 if s == 0 and any_before else None, jobs))
    if not project_next:
        steps.append(Step(None, [], (UNITS - 1, TILES - 1), UNITS - 1))
    return steps


def opening_steps():
    steps = [Step(jobs=[("weights", 0), ("x_load", 0)] + PROJECT_FIRST)]
    for step in range(LEAD):
        chain = [("max_split", 0), ("max_rows", 0)] if step == TILES else []
        steps.append(Step(maxima=max_tiles(step), jobs=chain))
    steps[-1].jobs.append(("warm", 0))
    return steps


def closing_steps():
    return [Step(jobs=j) for _, j in sorted(tail_jobs(1).items())]


class Segment:

    def __init__(self, steps):
        self.steps = steps
        self.total = dict.fromkeys(NAMES, 0)
        self.number = {}
        for n, step in enumerate(steps):
            if step.exp:
                for hh in range(GH):
                    self._count("score", ("exp", step.exp, hh))
            for tile in step.maxima:
                self._count("row", ("max", tile))
            if step.pv:
                self._count("pv", step.pv)
            if step.finished is not None:
                self._count("saved", step.finished)
            for job in step.jobs:
                for name, by in counts_of(job).items():
                    self._count(name, job, by)

    def _count(self, name, key, by=1):
        self.total[name] += by
        self.number[name, key] = self.total[name]

    def after(self, name, key):
        return self.base[name] + self.number.get((name, key), 0)


def build(nc, x, w, out):
    opening = Segment(opening_steps())
    first = Segment(batch_steps(True, False))
    middle = Segment(batch_steps(True, True))
    last = Segment(batch_steps(False, True))
    closing = Segment(closing_steps())
    loops = BATCH - 2

    def start_of(segment, i=0):
        before = {opening: [], first: [opening], middle: [opening, first], last: [opening, first] + [middle] * loops,
                  closing: [opening, first] + [middle] * loops + [last]}[segment]
        base = {n: sum(s.total[n] for s in before) for n in NAMES}
        if segment is middle:
            base = {n: i * middle.total[n] + base[n] if middle.total[n] else base[n] for n in NAMES}
        segment.base = base
        segment.opening, segment.closing = segment is opening, segment is closing
        segment.batch = {opening: -1, first: 0, middle: i + 1, last: BATCH - 1, closing: BATCH}[segment]

    def program(eng, emit):
        for segment in (opening, first):
            start_of(segment)
            emit(segment)
        with eng.Fori(0, loops) as i:
            start_of(middle, i)
            emit(middle)
        for segment in (last, closing):
            start_of(segment)
            emit(segment)

    def wait(eng, sem, count):
        if not isinstance(count, int) or count > 0:
            eng.wait_ge(sem, count)

    def last_of_group(i):
        return (GROUPS + i if i >= 0 else -1, TILES - 1)

    def alone(eng):
        eng.nop(nofuse=True)

    with ExitStack() as ctx:
        def sb(name, shape, dt):
            return ctx.enter_context(nc.sbuf_tensor(name, shape, dt))

        wt = sb("wt", [P, W_COLS], F32)
        ident_b = sb("ident_b", [P, P], BF16)
        w_ac = sb("w_ac", [P, 2 * CR], F32)
        b_ac = sb("b_ac", [P, 2], F32)
        wqs_s = sb("wqs_s", [P, P], F32)
        bqs_s = sb("bqs_s", [P, H], F32)
        bq_t = sb("bq_t", [P, 1], F32)
        x_in = sb("x_in", [P, TILES, D], F32)
        xT = sb("xT", [P, TOK], F32)
        k3v = sb("k3v", [P, TOK], F32)
        cross = sb("cross", [P, TOK], F32)
        val = [sb("q_val", [P, TOK], F32), sb("k_val", [P, TOK], F32), sb("kb_val", [P, TOK], F32)]
        parts = [sb("q_parts", [P, 3, TOK], BF16), sb("k_parts", [P, 3, TOK], BF16), sb("kb_parts", [P, 3, TOK], BF16)]
        rest = sb("rest", [P, TOK], F32)
        v_next = sb("v_next", [P, TILES, D], F32)
        v_cur = sb("v_cur", [P, TILES, H, VW], F32)
        q_op = sb("q_op", [P, H // 2, TOK], BF16)
        k_op = sb("k_op", [P, H // 2, TOK], BF16)
        probs = sb("probs", [P, 2, GH, HALF], F32)
        neg_max = sb("neg_max", [P, 2, GH, HT], F32)
        max_parts = sb("max_parts", [P, GH, 3, HT], BF16)
        max_rest = sb("max_rest", [P, 2, GH, HT], F32)
        max_row = sb("max_row", [GH * 3 * HT, P], BF16)
        attn = sb("attn", [P, 2, GROUPS, HALF], F32)
        recip = sb("recip", [P, HT, H], F32)
        o_tok = sb("o_tok", [P, HT, D], F32)
        oT = sb("oT", [P, HALF], F32)
        resid_in = sb("resid_in", [P, HT, D], F32)
        resid_bo = sb("resid_bo", [P, HT, D], F32)
        pre_ln = sb("pre_ln", [P, HT, D], F32)
        stats = sb("stats", [P, HT, 6], F32)
        mean_var = sb("mean_var", [P, HT, 2], F32)
        rstd = sb("rstd", [P, HT], F32)
        minus_half = sb("minus_half", [P, HT], F32)
        x1 = sb("x1", [P, HT, D], F32)
        x1_b2 = sb("x1_b2", [P, HT, D], F32)
        x1T = sb("x1T", [P, HALF], F32)
        hid = sb("hid", [P, FC, HALF], F32)
        y = sb("y", [P, HT, D], F32)

        row_bank = [ctx.enter_context(nc.psum_tensor(f"row_bank{i}", [P, TOK], F32)) for i in range(ROW_RING)]
        score_bank = [ctx.enter_context(nc.psum_tensor(f"score_bank{i}", [P, HALF], F32)) for i in range(SCORE_RING)]
        pv_bank = ctx.enter_context(nc.psum_tensor("pv_bank", [P, HALF], F32))

        stacked = [nc.dram_tensor(f"stacked_{n}", (P, 6, TOK), BF16, kind="Internal").ap() for n in "qk"]
        stacked_kb = nc.dram_tensor("stacked_kb", (H, 3, TOK), BF16, kind="Internal").ap()
        stacked_max = nc.dram_tensor("stacked_max", (2, GH * 3 * HT, P), BF16, kind="Internal").ap()

        S = {n: ctx.enter_context(nc.semaphore(n)) for n in
             ("w_first", "w_rest", "cleared", "v_zeroed", "prepared", "score_filled", "score_read", "row_filled", "row_read",
              "pv_done", "attn_saved", "x_loaded", "parts_split", "group0_stored", "group1_stored",
              "group2_stored", "group3_stored", "kb_stored", "group0_loaded", "group1_loaded",
              "group2_loaded", "group3_loaded", "values_staged", "max_split", "max_stored", "shift0_loaded",
              "shift1_loaded", "resid_loaded", "resid_biased", "ln_stats", "rstd_ready", "ln1_done", "x1_biased", "out_ready", "out_stored",
              "dve_step", "pool_step")}
        group_stored = [S[f"group{g}_stored"] for g in range(GROUPS)]
        group_loaded = [S[f"group{g}_loaded"] for g in range(GROUPS)]
        shift_loaded = [S["shift0_loaded"], S["shift1_loaded"]]

        def W(name, a=0, n=None, rows=slice(0, P)):
            at, width = _W[name]
            return wt[rows, at + a:at + (width if n is None else a + n)]

        def col(name, i=0, rows=slice(0, P)):
            return W("cols", COL[name] + i, 1, rows)

        def half_of(t, h):
            return t[:, h * HALF:(h + 1) * HALF]

        def by_tile(bank):
            return bank.rearrange("p (t d) -> p t d", d=D)

        def head_rows(hh):
            return 64 * (hh % 2), hh // 2

        block = ctx.enter_context(nc.Block())

        @block.tensor
        def _(pe):
            def emit(seg):
                def score_slot(key):
                    n = seg.number["score", key] - 1
                    wait(pe, S["score_read"], seg.base["score"] + max(n - SCORE_RING + 1, 0))
                    return score_bank[n % SCORE_RING]

                def row_slot(key):
                    n = seg.number["row", key] - 1
                    wait(pe, S["row_read"], seg.base["row"] + max(n - ROW_RING + 1, 0))
                    return row_bank[n % ROW_RING]

                def scores(u, c, hh):
                    r, pair = head_rows(hh)
                    qh, g = divmod(u, GROUPS)
                    bank = score_slot(("exp", (u, c), hh))
                    rows = slice(r, r + KS)
                    nc.tensor.matmul(bank[:], k_op[rows, 2 * g + pair, c * P:(c + 1) * P],
                                     q_op[rows, 2 * g + pair, qh * HALF:(qh + 1) * HALF],
                                     start=True, stop=True).then_inc(S["score_filled"], 1)

                def max_pass(tiles):
                    for tile in tiles:
                        unit, t, hh = tile
                        r, pair = head_rows(hh)
                        qh, g = divmod(unit % UNITS, GROUPS)
                        if t == 0 and hh == 0:
                            wait(pe, group_loaded[g], seg.after(f"loaded{g}", ("load_kb", g)) if unit >= UNITS
                                 or unit < 2 else seg.after(f"loaded{g}", ("load_kb", g - GROUPS)))
                        bank = row_slot(("max", tile))
                        q0 = qh * HALF + t * P
                        for kh in range(2):
                            mm = nc.tensor.matmul(half_of(bank, kh), q_op[r:r + KB, 2 * g + pair, q0:q0 + P],
                                                  half_of(k_op[r:r + KB, 2 * g + pair], kh), start=True, stop=True)
                            if kh:
                                mm.then_inc(S["row_filled"], 1)
                            yield

                def values(u, c):
                    g = u % GROUPS
                    wait(pe, S["score_read"], seg.after("score", ("exp", (u, c), GH - 1)))
                    if c == 0:
                        wait(pe, S["attn_saved"], seg.after("saved", u - 1))
                        if u < GROUPS:
                            wait(pe, S["values_staged"], seg.after("staged", ("stage_v", u - GROUPS)))
                    for hh in range(GH):
                        mm = nc.tensor.matmul(pv_bank[VW * hh:VW * (hh + 1), :], v_cur[:, c, GH * g + hh, :],
                                              probs[:, c % 2, hh, :], start=(c == 0), stop=(c == TILES - 1))
                    mm.then_inc(S["pv_done"], 1)

                def job(kind, i):
                    if kind == "weights":
                        pe.wait_ge(S["w_first"], 16)
                        bank = score_slot((kind, i))
                        for n, (a, s, b) in enumerate((("wk", "selAC", "bk"), ("wv", "selBD", "bv"))):
                            nc.tensor.matmul(bank[:, n * CR:(n + 1) * CR], W(a), W(s), start=True, stop=True)
                            mm = nc.tensor.matmul(bank[0:CR, 2 * CR + n:2 * CR + n + 1], W(s), col(b),
                                                  start=True, stop=True)
                        mm.then_inc(S["score_filled"], 1)
                    elif kind == "xT":
                        wait(pe, S["x_loaded"], seg.after("x", ("x_load", 0)))
                        bank = score_slot((kind, i))
                        for t in range(HT):
                            mm = nc.tensor.transpose(bank[:, t * P:(t + 1) * P], x_in[:, HT * i + t, :], W("ident"))
                        mm.then_inc(S["score_filled"], 1)
                    elif kind in ("q", "ac"):
                        wait(pe, S["score_read"], seg.after("score", ("xT", i)))
                        if kind == "ac" and seg.opening:
                            pe.wait_ge(S["score_read"], seg.after("score", ("weights", 0)))
                        bank = score_slot((kind, i))
                        lhs, rows = (W("wqT"), P) if kind == "q" else (w_ac[:, 0:CR], CR)
                        nc.tensor.matmul(bank[0:rows, :], lhs, half_of(xT, i), start=True,
                                         stop=True).then_inc(S["score_filled"], 1)
                    elif kind == "bd":
                        bank = row_slot((kind, i))
                        nc.tensor.matmul(bank[0:CR, 0:HALF], w_ac[:, CR:2 * CR], half_of(xT, i), start=True,
                                         stop=True).then_inc(S["row_filled"], 1)
                    elif kind == "k":
                        wait(pe, S["row_read"], seg.after("row", ("bd", i)))
                        if seg.opening and i == 0:
                            pe.wait_ge(S["prepared"], 5)
                        bank = score_slot((kind, i))
                        nc.tensor.matmul(bank[:], W("wkT"), half_of(xT, i), start=True, stop=False)
                        nc.tensor.matmul(bank[:], wqs_s[0:CR, :], half_of(cross[0:CR], i), start=False,
                                         stop=True).then_inc(S["score_filled"], 1)
                    elif kind == "kbias":
                        bank = score_slot((kind, i))
                        nc.tensor.matmul(bank[0:H, :], bqs_s[0:CR, :], half_of(cross[0:CR], i), start=True,
                                         stop=True).then_inc(S["score_filled"], 1)
                    elif kind == "v":
                        if seg.opening:
                            pe.wait_ge(S["w_rest"], 16)
                        bank = by_tile(row_slot((kind, i))[:])
                        for t in range(TILES):
                            mm = nc.tensor.matmul(bank[:, t, :], xT[:, t * P:(t + 1) * P], W("wvT"),
                                                  start=True, stop=True)
                        mm.then_inc(S["row_filled"], 1)
                    elif kind == "max_rows":
                        wait(pe, S["max_split"], seg.after("max_split", ("max_split", i)))
                        bank = row_slot((kind, i))[:].bitcast(BF16)
                        alone(pe)
                        nc.tensor.transpose(bank[0:GH * 3 * HT, 0:P], max_parts[:].rearrange("p h r t -> p (h r t)"),
                                            ident_b[:]).then_inc(S["row_filled"], 1)
                    elif kind == "norm":
                        half, t = i
                        wait(pe, S["attn_saved"], seg.after("saved", GROUPS - 1 if half == 0 else -1))
                        bank = by_tile(row_slot((kind, i))[:])
                        for g in range(GROUPS):
                            mm = nc.tensor.transpose(bank[:, g, :], attn[:, half, g, t * P:(t + 1) * P], W("ident"))
                        mm.then_inc(S["row_filled"], 1)
                    elif kind == "warm":
                        for _ in range(WARMING):
                            nc.tensor.matmul(pv_bank[:], ident_b[:], half_of(parts[0][:, 0, :], 0),
                                             start=True, stop=True)
                    elif kind == "oT":
                        wait(pe, S["row_read"], seg.after("row", ("norm", (i, HT - 1))))
                        bank = score_slot((kind, i))
                        for t in range(HT):
                            mm = nc.tensor.transpose(bank[:, t * P:(t + 1) * P], o_tok[:, t, :], W("ident"))
                        mm.then_inc(S["score_filled"], 1)
                    elif kind == "wo":
                        wait(pe, S["score_read"], seg.after("score", ("oT", i)))
                        bank = by_tile(row_slot((kind, i))[:])
                        for t in range(HT):
                            mm = nc.tensor.matmul(bank[:, t, :], oT[:, t * P:(t + 1) * P], W("woT"),
                                                  start=True, stop=True)
                        mm.then_inc(S["row_filled"], 1)
                    elif kind == "x1T":
                        wait(pe, S["ln1_done"], seg.after("ln1", ("stats1", i)))
                        bank = score_slot((kind, i))
                        for t in range(HT):
                            mm = nc.tensor.transpose(bank[:, t * P:(t + 1) * P], x1[:, t, :], W("ident"))
                        mm.then_inc(S["score_filled"], 1)
                    elif kind == "ffn1":
                        half, c = i
                        wait(pe, S["score_read"], seg.after("score", ("x1T", half)))
                        bank = score_slot((kind, i))
                        nc.tensor.matmul(bank[:], W("w1", c * P, P), x1T[:], start=True,
                                         stop=True).then_inc(S["score_filled"], 1)
                    elif kind == "ffn2":
                        wait(pe, S["score_read"], seg.after("score", ("ffn1", (i, FC - 1))))
                        bank = by_tile(row_slot((kind, i))[:])
                        for t in range(HT):
                            for c in range(FC):
                                mm = nc.tensor.matmul(bank[:, t, :], hid[:, c, t * P:(t + 1) * P], W("w2", c * P, P),
                                                      start=(c == 0), stop=(c == FC - 1))
                        mm.then_inc(S["row_filled"], 1)

                for step in seg.steps:
                    rows = max_pass(step.maxima)
                    if step.exp:
                        u, c = step.exp
                        if c == 0:
                            key = ("max_rows", u)
                            wait(pe, shift_loaded[u % 2], seg.after(f"shift{u % 2}", key))
                        for hh in range(GH):
                            scores(u, c, hh)
                            next(rows, None)
                    for _ in rows:
                        pass
                    if step.pv:
                        values(*step.pv)
                    for kind, i in step.jobs:
                        job(kind, i)

            program(pe, emit)

        @block.scalar
        def _(act):
            def emit(seg):
                def filled(key):
                    n = seg.number["score", key] - 1
                    wait(act, S["score_filled"], seg.base["score"] + n + 1)
                    return score_bank[n % SCORE_RING]

                def job(kind, i):
                    if kind == "weights":
                        bank = filled((kind, i))
                        nc.scalar.activation(w_ac[:], bank[:, 0:2 * CR], ACT.Identity)
                        nc.scalar.activation(b_ac[0:CR, 0:1], bank[0:CR, 2 * CR:2 * CR + 1], ACT.Identity,
                                             bias=col("bksAC", rows=slice(0, CR)))
                        nc.scalar.activation(b_ac[0:CR, 1:2], bank[0:CR, 2 * CR + 1:2 * CR + 2], ACT.Identity,
                                             bias=col("bvsBD", rows=slice(0, CR))).then_inc(S["score_read"], 1)
                    elif kind == "xT":
                        bank = filled((kind, i))
                        nc.scalar.activation(half_of(xT, i), bank[:], ACT.Identity).then_inc(S["score_read"], 1)
                    elif kind == "ac":
                        bank = filled((kind, i))
                        if seg.opening and i == 0:
                            act.wait_ge(S["score_read"], seg.after("score", ("weights", 0)))
                        nc.scalar.activation(half_of(k3v[0:CR], i), bank[0:CR, :], ACT.Identity,
                                             bias=b_ac[0:CR, 0:1]).then_inc(S["score_read"], 1)
                    elif kind in ("q", "k", "kbias"):
                        bank = filled((kind, i))
                        which = ("q", "k", "kbias").index(kind)
                        if i == 0:
                            wait(act, S["parts_split"], seg.base["split"])
                        if kind == "q":
                            if seg.opening and i == 0:
                                act.wait_ge(S["prepared"], 1)
                            nc.scalar.activation(half_of(val[0], i), bank[:], ACT.Identity, scale=col("temp"),
                                                 bias=bq_t[:]).then_inc(S["score_read"], 1)
                        elif kind == "k":
                            nc.scalar.activation(half_of(val[1], i), bank[:], ACT.Identity,
                                                 bias=col("bk")).then_inc(S["score_read"], 1)
                        else:
                            nc.scalar.activation(half_of(val[2][0:H], i), bank[0:H, :],
                                                 ACT.Identity).then_inc(S["score_read"], 1)
                    elif kind == "oT":
                        bank = filled((kind, i))
                        nc.scalar.activation(oT[:], bank[:], ACT.Identity).then_inc(S["score_read"], 1)
                    elif kind == "x1T":
                        bank = filled((kind, i))
                        nc.scalar.activation(x1T[:], bank[:], ACT.Identity).then_inc(S["score_read"], 1)
                    elif kind == "ffn1":
                        bank = filled((kind, i))
                        nc.scalar.activation(hid[:, i[1], :], bank[:], ACT.Relu,
                                             bias=col("b1", i[1])).then_inc(S["score_read"], 1)

                for step in seg.steps:
                    if step.exp:
                        u, c = step.exp
                        wait(act, S["pv_done"], seg.after("pv", divmod(TILES * u + c - 2, TILES)))
                        for hh in range(GH):
                            bank = filled(("exp", (u, c), hh))
                            nc.scalar.activation(probs[:, c % 2, hh, :], bank[:], ACT.Exp).then_inc(S["score_read"], 1)
                    if step.finished is not None:
                        wait(act, S["pv_done"], seg.after("pv", step.pv))
                        qh, g = divmod(step.finished % UNITS, GROUPS)
                        nc.scalar.activation(attn[:, qh, g, :], pv_bank[:], ACT.Identity).then_inc(S["attn_saved"], 1)
                    for kind, i in step.jobs:
                        job(kind, i)

            act.wait_ge(S["w_first"], 16)
            program(act, emit)

        @block.vector
        def _(dve):
            done = [0]

            def emit(seg):
                done[0] = 0

                def then(ins):
                    done[0] += 1
                    ins.then_inc(S["dve_step"], 1)
                    dve.wait_ge(S["dve_step"], seg.base["dve_step"] + done[0])

                def filled(key):
                    n = seg.number["row", key] - 1
                    wait(dve, S["row_filled"], seg.base["row"] + n + 1)
                    return row_bank[n % ROW_RING]

                def statistics(tiles):
                    for t in tiles:
                        last = nc.vector.bn_stats(stats[:, t, :], pre_ln[:, t, :])
                    return last

                def mean_and_variance(to, done_sem):
                    then(statistics(range(HT // 2, HT)))
                    alone(dve)
                    for t in range(HT):
                        last = nc.vector.bn_aggr(mean_var[:, t, :], stats[:, t, :])
                    last.then_inc(S["ln_stats"], 1)
                    if seg.closing:
                        dve.wait_ge(S["rstd_ready"], 1 if to is x1 else 2)
                        if to is y:
                            dve.wait_ge(S["out_stored"], seg.base["out_stored"])
                        for t in range(HT):
                            last = nc.vector.tensor_scalar(to[:, t, :], pre_ln[:, t, :], mean_var[:, t, 0:1],
                                                           rstd[:, t:t + 1], ALU.subtract, ALU.mult)
                        last.then_inc(done_sem, 1)

                def job(kind, i):
                    if kind == "bd":
                        bank = filled((kind, i))
                        dve.wait_ge(S["score_read"], seg.after("score", ("ac", i)))
                        nc.vector.scalar_tensor_tensor(out=half_of(cross[0:CR], i), in0=bank[0:CR, 0:HALF],
                                                       scalar=b_ac[0:CR, 1:2], in1=half_of(k3v[0:CR], i),
                                                       op0=ALU.add, op1=ALU.mult).then_inc(S["row_read"], 1)
                    elif kind == "split_first":
                        which, half = i
                        rows, name = ((P, "q"), (P, "k"), (H, "kbias"))[which]
                        cols = slice(0, TOK) if half is None else slice(HALF * half, HALF * (half + 1))
                        v, part, r = val[which][0:rows, cols], parts[which][0:rows, :, cols], rest[0:rows, cols]
                        dve.wait_ge(S["score_read"], seg.after("score", (name, 1 if half is None else half)))
                        wait(dve, S["parts_split"], seg.after("split", (kind, i)) - 1)
                        then(nc.vector.tensor_copy(part[:, 0, :], v))
                        then(nc.vector.tensor_tensor(r, v, part[:, 0, :], ALU.subtract))
                        then(nc.vector.tensor_copy(part[:, 1, :], r))
                        nc.vector.tensor_tensor(part[:, 2, :], r, part[:, 1, :],
                                                ALU.subtract).then_inc(S["parts_split"], 1)
                    elif kind == "v":
                        bank = filled((kind, i))
                        wait(dve, S["values_staged"], seg.after("staged", ("stage_v", -1)))
                        bv = W("bv_row").unsqueeze(1).broadcast_to([P, TILES, D])
                        nc.vector.tensor_tensor(v_next[:], by_tile(bank[:]), bv, ALU.add).then_inc(S["row_read"], 1)
                    elif kind == "max_split":
                        buf = i % 2
                        tile = ("max", (i, HT - 1, GH - 1))
                        dve.wait_ge(S["row_read"], seg.after("row", tile))
                        nm, r = neg_max[:, buf], max_rest
                        then(nc.vector.tensor_copy(max_parts[:, :, 0, :], nm))
                        then(nc.vector.tensor_tensor(r[:, 0], nm, max_parts[:, :, 0, :], ALU.subtract))
                        then(nc.vector.tensor_copy(max_parts[:, :, 1, :], r[:, 0]))
                        nc.vector.tensor_tensor(max_parts[:, :, 2, :], r[:, 0], max_parts[:, :, 1, :],
                                                ALU.subtract).then_inc(S["max_split"], 1)
                    elif kind == "max_rows":
                        bank = filled((kind, i))
                        wait(dve, S["max_stored"], seg.after("max_stored", (kind, i)) - 16)
                        nc.vector.tensor_copy(max_row[:], bank[:].bitcast(BF16)[0:GH * 3 * HT, 0:P])\
                            .then_inc(S["row_read"], 1)
                    elif kind == "norm":
                        bank = filled((kind, i))
                        heads = bank[:, 0:GROUPS * P].rearrange("p (h r) -> p h r", r=VW)
                        then(nc.vector.reciprocal(recip[:, i[1], :], heads[:, :, HD]))
                        nc.vector.tensor_tensor(o_tok[:, i[1], :].rearrange("p (h d) -> p h d", d=HD),
                                                heads[:, :, 0:HD], recip[:, i[1], :].unsqueeze(2).broadcast_to([P, H, HD]),
                                                ALU.mult).then_inc(S["row_read"], 1)
                    elif kind == "wo":
                        bank = filled((kind, i))
                        wait(dve, S["resid_biased"], seg.after("resid_bo", ("resid", i)))
                        wait(dve, S["out_ready"], seg.after("out", ("stats2", i)) - 1)
                        b = by_tile(bank[:, 0:HALF])
                        nc.vector.tensor_tensor(pre_ln[:], b, resid_bo[:], ALU.add).then_inc(S["row_read"], 1)
                        dve.wait_ge(S["row_read"], seg.after("row", (kind, i)))
                        statistics(range(HT // 2))
                    elif kind == "ffn2":
                        bank = filled((kind, i))
                        wait(dve, S["x1_biased"], seg.after("x1_b2", ("stats1", i)))
                        b = by_tile(bank[:, 0:HALF])
                        nc.vector.tensor_tensor(pre_ln[:], b, x1_b2[:], ALU.add).then_inc(S["row_read"], 1)
                        dve.wait_ge(S["row_read"], seg.after("row", (kind, i)))
                        statistics(range(HT // 2))
                    elif kind == "stats1":
                        mean_and_variance(x1, S["ln1_done"])
                    elif kind == "stats2":
                        mean_and_variance(y, S["out_ready"])

                for step in seg.steps:
                    for tile in step.maxima:
                        unit, t, hh = tile
                        bank = filled(("max", tile))
                        nc.vector.tensor_reduce(neg_max[:, unit % 2, hh, t:t + 1], bank[:], AX_X, ALU.max,
                                                negate=True).then_inc(S["row_read"], 1)
                    for kind, i in step.jobs:
                        job(kind, i)
                    
            nc.vector.memset(k_op[:].rearrange("p a t -> p (a t)").bitcast(F32), TWO_ONES).then_inc(S["cleared"], 1)
            dve.wait_ge(S["w_first"], 16)
            nc.vector.tensor_scalar(bq_t[:], col("bq"), col("temp"), None, ALU.mult).then_inc(S["prepared"], 1)
            nc.vector.tensor_copy(ident_b[:], W("ident")).then_inc(S["prepared"], 1)
            dve.wait_ge(S["w_rest"], 16)
            nc.vector.tensor_scalar(wqs_s[0:CR], W("wqs", rows=slice(0, CR)), col("sign", rows=slice(0, CR)), None,
                                    ALU.mult).then_inc(S["prepared"], 1)
            nc.vector.tensor_scalar(bqs_s[0:CR], W("bqs", rows=slice(0, CR)), col("sign", rows=slice(0, CR)),
                                    col("temp", rows=slice(0, CR)), ALU.mult, ALU.mult).then_inc(S["prepared"], 1)
            nc.vector.memset(minus_half[:], -0.5).then_inc(S["prepared"], 1)
            program(dve, emit)

        @block.gpsimd
        def _(pool):
            def emit(seg):
                done = [0]

                def then(ins):
                    done[0] += 1
                    ins.then_inc(S["pool_step"], 1)
                    pool.wait_ge(S["pool_step"], seg.base["pool_step"] + done[0])
                    alone(pool)

                def normalise(to, key):
                    pool.wait_ge(S["ln_stats"], seg.after("ln_stats", key))
                    alone(pool)
                    then(nc.gpsimd.tensor_scalar(rstd[:], mean_var[:, :, 1], EPS, None, ALU.add))
                    power = nc.gpsimd.tensor_tensor(rstd[:], rstd[:], minus_half[:], ALU.pow)
                    if seg.closing:
                        power.then_inc(S["rstd_ready"], 1)
                        return None
                    then(power)
                    for t in range(HT):
                        last = nc.gpsimd.tensor_scalar(to[:, t, :], pre_ln[:, t, :], mean_var[:, t, 0:1],
                                                       rstd[:, t:t + 1], ALU.subtract, ALU.mult)
                    return last

                def job(kind, i):
                    if kind == "split":
                        rows = H if i == 2 else P
                        v, part, r = val[i][0:rows, :], parts[i], rest[0:rows, :]
                        pool.wait_ge(S["score_read"], seg.after("score", (("q", "k", "kbias")[i], 1)))
                        alone(pool)
                        for g in range(GROUPS):
                            wait(pool, group_stored[g], seg.base[f"stored{g}"])
                            alone(pool)
                        wait(pool, S["kb_stored"], seg.base["kb_stored"])
                        alone(pool)
                        then(nc.gpsimd.tensor_copy(part[0:rows, 0, :], v))
                        then(nc.gpsimd.tensor_tensor(r, v, part[0:rows, 0, :], ALU.subtract))
                        then(nc.gpsimd.tensor_copy(part[0:rows, 1, :], r))
                        nc.gpsimd.tensor_tensor(part[0:rows, 2, :], r, part[0:rows, 1, :],
                                                ALU.subtract).then_inc(S["parts_split"], 1)
                    elif kind == "stage_v":
                        pool.wait_ge(S["row_read"], seg.after("row", ("v", min(i, 0))))
                        if not seg.opening:
                            pool.wait_ge(S["pv_done"], seg.after("pv", last_of_group(i)))
                        alone(pool)
                        g = i % GROUPS
                        heads = slice(GH * g, GH * (g + 1))
                        nc.gpsimd.tensor_copy(v_cur[:, :, heads, 0:HD],
                                              v_next[:].rearrange("p t (h d) -> p t h d", d=HD)[:, :, heads, :])\
                            .then_inc(S["values_staged"], 1)
                    elif kind == "resid":
                        wait(pool, S["resid_loaded"], seg.after("resid", (kind, i)))
                        wait(pool, S["ln1_done"], seg.after("ln1", ("stats1", i)) - 1)
                        nc.gpsimd.tensor_tensor(resid_bo[:], resid_in[:],
                                                W("bo_row").unsqueeze(1).broadcast_to([P, HT, D]),
                                                ALU.add).then_inc(S["resid_biased"], 1)
                    elif kind == "stats1":
                        last = normalise(x1, (kind, i))
                        if last:
                            last.then_inc(S["ln1_done"], 1)
                        pool.wait_ge(S["ln1_done"], seg.after("ln1", (kind, i)))
                        nc.gpsimd.tensor_tensor(x1_b2[:], x1[:], W("b2_row").unsqueeze(1).broadcast_to([P, HT, D]),
                                                ALU.add).then_inc(S["x1_biased"], 1)
                    elif kind == "stats2":
                        wait(pool, S["out_stored"], seg.after("out_stored", (kind, i)) - 16)
                        last = normalise(y, (kind, i))
                        if last:
                            last.then_inc(S["out_ready"], 1)

                for step in seg.steps:
                    for kind, i in step.jobs:
                        job(kind, i)

            nc.gpsimd.memset(q_op[:].rearrange("p a t -> p (a t)").bitcast(F32), TWO_ONES).then_inc(S["cleared"], 1)
            nc.gpsimd.memset(v_cur[:].rearrange("p c h w -> p (c h w)"), 0.0).then_inc(S["v_zeroed"], 1)
            pool.wait_ge(S["v_zeroed"], 1)
            nc.gpsimd.memset(v_cur[:].rearrange("p c h w -> p (c h) w")[:, :, HD:HD + 1], 1.0).then_inc(S["cleared"], 1)
            pool.wait_ge(S["w_rest"], 16)
            pool.wait_ge(S["cleared"], 3)
            pool.wait_ge(S["prepared"], 5)
            program(pool, emit)

        @block.sync
        def _(sp):
            def batch_rows(t, b, half=None):
                rows = t[bass.ds(b, 1)].rearrange("b (t p) d -> p (b t) d", p=P)
                return rows if half is None else rows[:, half * HT:(half + 1) * HT, :]

            def emit(seg):
                def job(kind, i):
                    if kind == "x_load":
                        wait(sp, S["score_filled"], seg.base["score"])
                        alone(sp)
                        if seg.opening:
                            return
                        sp.dma_start(x_in[:], batch_rows(x, seg.batch + 1)).then_inc(S["x_loaded"], 16)
                    elif kind == "store":
                        wait(sp, group_loaded[i], seg.after(f"loaded{i}", ("load_kb", i - GROUPS)))
                        alone(sp)
                        rows = slice(GH * HD * i, GH * HD * (i + 1))
                        for op in range(2):
                            split = ("split_first", ((0, None), (1, 1))[op]) if seg.opening else ("split", op)
                            sp.wait_ge(S["parts_split"], seg.after("split", split))
                            alone(sp)
                            for n, slots in ((0, slice(0, 3)), (1, slice(3, 5)), (2, slice(5, 6))):
                                width = slots.stop - slots.start
                                if op == 0:
                                    part = parts[0][rows, n, :].unsqueeze(1).broadcast_to([GH * HD, width, TOK])
                                else:
                                    part = parts[1][rows, 0:width, :]
                                sp.dma_start(stacked[op][rows, slots, :], part).then_inc(group_stored[i], 16)
                    elif kind == "store_kb":
                        sp.wait_ge(S["parts_split"], seg.after("split", ("split_first", (2, None)) if seg.opening
                                                               else ("split", 2)))
                        alone(sp)
                        for g in range(GROUPS):
                            wait(sp, group_loaded[g], seg.after(f"loaded{g}", ("load_kb", g - GROUPS)))
                            alone(sp)
                        sp.dma_start(stacked_kb, parts[2][0:H]).then_inc(S["kb_stored"], 16)
                    elif kind == "load":
                        g = i % GROUPS
                        sp.wait_ge(group_stored[g], seg.after(f"stored{g}", ("store", i)))
                        alone(sp)
                        if not seg.opening:
                            sp.wait_ge(S["pv_done"], seg.after("pv", last_of_group(i)))
                        for j in range(2):
                            heads = slice(GH * g + j, GH * (g + 1), 2)
                            pairs = slice(2 * g, 2 * g + 2)
                            for op, src in ((q_op, stacked[0]), (k_op, stacked[1])):
                                by_head = src.rearrange("(h d) s t -> h (d s) t", d=HD)
                                sp.dma_start(op[64 * j:64 * j + KM, pairs, :],
                                             by_head[heads].rearrange("h r t -> r h t"))\
                                    .then_inc(group_loaded[g], 16)
                    elif kind == "load_kb":
                        sp.wait_ge(S["kb_stored"], seg.after("kb_stored", ("store_kb", min(i, 0))))
                        alone(sp)
                        g = i % GROUPS
                        for j in range(2):
                            heads = slice(GH * g + j, GH * (g + 1), 2)
                            sp.dma_start(k_op[64 * j + KM:64 * j + KB, 2 * g:2 * g + 2, :],
                                         stacked_kb[heads].rearrange("h r t -> r h t")).then_inc(group_loaded[g], 16)
                    elif kind == "max_rows":
                        sp.wait_ge(S["row_read"], seg.after("row", (kind, i)))
                        sp.dma_start(stacked_max[i % 2], max_row[:]).then_inc(S["max_stored"], 16)
                        sp.wait_ge(S["max_stored"], seg.after("max_stored", (kind, i)))
                        qh, g = divmod(i % UNITS, GROUPS)
                        by_row = stacked_max[i % 2].rearrange("(a j r t) q -> a j r (t q)", a=2, j=2, r=3)
                        for j in range(2):
                            sp.dma_start(q_op[64 * j + KB:64 * j + KS, 2 * g:2 * g + 2, qh * HALF:(qh + 1) * HALF],
                                         by_row[:, j].rearrange("a r q -> r a q")).then_inc(shift_loaded[i % 2], 16)
                    elif kind == "resid":
                        wait(sp, S["resid_biased"], seg.after("resid_bo", (kind, i)) - 1)
                        alone(sp)
                        b = seg.batch - 1 if i == 1 else seg.batch
                        sp.dma_start(resid_in[:], batch_rows(x, b, i)).then_inc(S["resid_loaded"], 16)
                    elif kind == "stats2":
                        sp.wait_ge(S["out_ready"], seg.after("out", (kind, i)))
                        alone(sp)
                        b = seg.batch - 1 if i == 1 else seg.batch
                        sp.dma_start(batch_rows(out, b, i), y[:]).then_inc(S["out_stored"], 16)

                for step in seg.steps:
                    for kind, i in step.jobs:
                        job(kind, i)

            sp.dma_start(wt[:, 0:W_FIRST], w[:, 0:W_FIRST]).then_inc(S["w_first"], 16)
            sp.dma_start(x_in[:], batch_rows(x, 0)).then_inc(S["x_loaded"], 16)
            sp.dma_start(wt[:, W_FIRST:], w[:, W_FIRST:]).then_inc(S["w_rest"], 16)
            sp.wait_ge(S["cleared"], 3)
            program(sp, emit)
            sp.wait_ge(S["out_stored"], closing.after("out_stored", ("stats2", 1)))


def pack(i):
    f = np.float32
    Wks, Wvs, Wqs = (np.asarray(i["L0_attn_" + n], f) for n in ("Wks", "Wvs", "Wqs"))
    bks, bvs, bqs = (np.asarray(i["L0_attn_" + n], f) for n in ("bks", "bvs", "bqs"))
    get = lambda n: np.asarray(i["L0_attn_" + n], f)
    w = np.zeros((P, W_COLS), f)

    def put(name, a, at=0):
        a = np.atleast_2d(a)
        w[0:a.shape[0], _W[name][0] + at:_W[name][0] + at + a.shape[1]] = a

    put("ident", np.eye(P, dtype=f))
    put("wqT", get("Wq").T), put("wkT", get("Wk").T), put("wvT", get("Wv").T), put("woT", get("Wo").T)
    put("wk", get("Wk")), put("wv", get("Wv"))
    for h in range(H):
        for c in range(3):
            for at, kc, vc in ((0, (c + 1) % 3, (c + 2) % 3), (64, (c + 2) % 3, (c + 1) % 3)):
                r = at + 3 * h + c
                w[HD * h:HD * (h + 1), _W["selAC"][0] + r] = Wks[kc]
                w[HD * h:HD * (h + 1), _W["selBD"][0] + r] = Wvs[vc]
                w[r, _W["cols"][0] + COL["bksAC"]] = bks[kc]
                w[r, _W["cols"][0] + COL["bvsBD"]] = bvs[vc]
                w[r, _W["wqs"][0] + HD * h:_W["wqs"][0] + HD * (h + 1)] = Wqs[c]
                w[r, _W["bqs"][0] + h] = bqs[c]
    for name in ("bq", "bk", "bv"):
        put("cols", get(name)[:, None], COL[name])
    put("cols", np.full((P, 1), get("temp"), f), COL["temp"])
    put("cols", np.where(np.arange(P) < 64, 1, -1).astype(f)[:, None], COL["sign"])
    put("cols", np.asarray(i["L0_ffn_b1"], f).reshape(FC, P).T, COL["b1"])
    for name, b in (("bv_row", get("bv")), ("bo_row", get("bo")), ("b2_row", np.asarray(i["L0_ffn_b2"], f))):
        put(name, np.broadcast_to(b, (P, D)))
    put("w1", np.asarray(i["L0_ffn_W1"], f))
    put("w2", np.asarray(i["L0_ffn_W2"], f).reshape(FC, P, D).transpose(1, 0, 2).reshape(P, FC * D))
    return w


def kernel(**inputs):
    import concourse.bacc as bacc
    from concourse.bass_utils import run_bass_kernel_spmd

    nc = bacc.Bacc("TRN2", target_bir_lowering=False, num_devices=1)
    arrays = {"x": np.ascontiguousarray(inputs["L0_attn_x"]), "weights": pack(inputs)}
    x, w = (nc.dram_tensor(n, a.shape, F32, kind="ExternalInput").ap() for n, a in arrays.items())
    out = nc.dram_tensor("out", (BATCH, TOK, D), F32, kind="ExternalOutput").ap()
    build(nc, x, w, out)
    return run_bass_kernel_spmd(nc, [arrays], core_ids=[0]).results[0]["out"]
```

```python
from contextlib import ExitStack

import numpy as np
import concourse.bass as bass
from concourse import mybir

F32 = mybir.dt.float32
BF16 = mybir.dt.bfloat16
ACT = mybir.ActivationFunctionType
ALU = mybir.AluOpType
AX_X = mybir.AxisListType.X

BATCH, TOK, D, H = 4, 1024, 128, 16
HD = D // H
INTER = 512
P = 128
HALF = TOK // 2
TILES = TOK // P
HT = HALF // P
GROUPS = 4
GH = H // GROUPS
UNITS = 2 * GROUPS
FC = INTER // P
KM = 6 * HD
KB = KM + 3
KS = KB + 3
FIRST_WARMING, WHILE_SPLIT, WARMING, KEEPING_WARM, WHILE_NORM = 8, 5, 10, 4, 22
C3 = 3 * H
CR = 64 + C3
VW = 32
EPS = 1e-5
TWO_ONES = float(np.array([0x3F803F80], np.uint32).view(np.float32)[0])
SCORE_RING, ROW_RING = 3, 2

_W = {}
_at = 0
for _name, _width in (
    ("ident", P), ("wqT", P), ("wkT", P), ("wk", P), ("wv", P), ("selAC", CR), ("selBD", CR), ("cols", 16),
    ("wvT", P), ("wqs", P), ("bqs", H), ("bv_row", P), ("woT", P), ("bo_row", P), ("b2_row", P),
    ("w1", INTER), ("w2", INTER)):
    _W[_name] = (_at, _width)
    _at += _width
W_COLS = _at
W_FIRST = _W["wvT"][0]
COL = {"bq": 0, "bk": 1, "bv": 2, "bksAC": 3, "bvsBD": 4, "temp": 5, "sign": 6, "b1": 7}

COUNTS = {
    "weights": {"score": 1},
    "x_load": {"x": 16},
    "ac": {"score": 1},
    "bd": {"row": 1},
    "q": {"score": 1},
    "k": {"score": 1},
    "kbias": {"score": 1},
    "v": {"row": 1},
    "split": {"split": 1, "pool_step": 3},
    "split_first": {"split": 1, "dve_step": 3},
    "store_kb": {"kb_stored": 32},
    "stage_v": {"staged": 1},
    "max_split": {"max_split": 1, "dve_step": 3},
    "max_rows": {"score": 1, "max_stored": 16},
    "resid": {"resid": 16, "resid_bo": 1},
    "norm": {"row": 1, "dve_step": 1},
    "warm": {},
    "oT": {"score": 1},
    "wo": {"row": 1},
    "stats1": {"dve_step": 1, "ln_stats": 1, "pool_step": 2, "ln1": 1, "x1_b2": 1},
    "x1T": {"score": 1},
    "ffn1": {"score": 1},
    "ffn2": {"row": 1},
    "stats2": {"dve_step": 1, "ln_stats": 1, "pool_step": 2, "out": 1, "out_stored": 16},
}
NAMES = ("score", "row", "pv", "saved", "x", "split", "stored0", "stored1", "stored2", "stored3", "kb_stored", "loaded0", "loaded1", "loaded2", "loaded3",
         "staged", "max_split", "max_stored", "shift0", "shift1", "resid", "resid_bo", "ln_stats", "ln1", "x1_b2", "out",
         "out_stored", "dve_step", "pool_step")
LOAD_DMAS, LOAD_KB_DMAS, SHIFT_DMAS, STORE_DMAS = 4, 2, 2, 6
KB_AT = 32
KB_ROWS = KB_AT + H
LEAD = 12
OPENING_LEAD = 10
HEAD_ORDER = (0, 2, 1, 3)
LAST_HEAD = HEAD_ORDER[-1]


def counts_of(job):
    kind, i = job[0], job[1]
    if kind == "store":
        return {f"stored{i}": 16 * STORE_DMAS}
    if kind == "load":
        return {f"loaded{i % GROUPS}": 16 * LOAD_DMAS}
    if kind == "load_kb":
        return {f"loaded{i % GROUPS}": 16 * LOAD_KB_DMAS}
    if kind == "max_rows":
        return COUNTS[kind] | {f"shift{i % 2}": 16 * SHIFT_DMAS}
    return COUNTS[kind]


def tail_jobs(half):
    jobs = {(0, 0): [("resid", half)], (0, 6): [("oT", half)], (0, 7): [("wo", half)], (1, 0): [("stats1", half)],
            (1, 3): [("x1T", half)], (3, 0): [("ffn2", (half, 0))], (3, 1): [("ffn2", (half, 1))],
            (3, 2): [("stats2", half)]}
    for t in range(HT):
        jobs[(0, 1 + t)] = [("norm", (half, t))]
    for c, at in enumerate(((1, 4), (1, 5), (2, 4), (2, 5))):
        jobs[at] = [("ffn1", (half, c))]
    return jobs


PROJECT = {(0, 0): [("x_load", 0)], (0, 6): [("ac", 0)], (1, 1): [("q", 0)], (1, 2): [("q", 1)],
           (1, 3): [("split", 0)], (1, 5): [("ac", 1)], (1, 7): [("bd", 0)], (2, 2): [("bd", 1)],
           (2, 3): [("k", 0)], (2, 6): [("k", 1)], (2, 7): [("split", 1)], (3, 4): [("kbias", 0)],
           (3, 5): [("split", 2)], (3, 6): [("v", 0)],
           (4, 6): [("store", 0), ("store_kb", 0)], (4, 7): [("store", 1)], (5, 2): [("store", 2)], (5, 3): [("store", 3)]}
PROJECT_FIRST = [("q", 0), ("q", 1), ("split_first", (0, 0)), ("ac", 0), ("ac", 1), ("bd", 0),
                 ("bd", 1), ("split_first", (0, 1)), ("k", 0), ("k", 1), ("kbias", 0), ("split_first", (1, 0)),
                 ("split_first", (1, 1)), ("split_first", (2, 0)), ("store", 0), ("store_kb", 0), ("load", 0),
                 ("load_kb", 0), ("store", 1), ("load", 1), ("load_kb", 1), ("store", 2), ("load", 2), ("load_kb", 2),
                 ("store", 3), ("load", 3), ("load_kb", 3), ("v", 0), ("stage_v", 0), ("stage_v", 1), ("stage_v", 2),
                 ("stage_v", 3)]


class Step:
    def __init__(self, exp=None, maxima=(), pv=None, finished=None, jobs=()):
        self.exp, self.maxima, self.pv, self.finished, self.jobs = exp, list(maxima), pv, finished, list(jobs)


def max_tiles(first, last):
    return [(n // (2 * TILES), n % (2 * TILES) // GH, n % GH ^ 1) for n in range(first, last)]


def tiles_before(n, catching_up=False):
    due = 2 * (n + LEAD)
    return min(due, 2 * OPENING_LEAD + 3 * n) if catching_up else due


def batch_steps(project_next, tail_before):
    steps = []
    for u in range(UNITS):
        for s in range(TILES):
            jobs = []
            if s == 4 and (u + 1 < UNITS or project_next):
                jobs.append(("max_split", u + 1))
            if s == 5 and (u + 1 < UNITS or project_next):
                jobs.append(("max_rows", u + 1))
            if not tail_before and (u, s) == (0, 0):
                jobs.append(("warm", KEEPING_WARM))
            if tail_before and (u, s) == (0, 1):
                jobs += [("load", -1), ("load_kb", -1), ("stage_v", -1)]
            if tail_before:
                jobs += tail_jobs(1).get((u, s), [])
            jobs += tail_jobs(0).get((u - GROUPS, s), [])
            if project_next:
                jobs += PROJECT.get((u, s), [])
                if u > GROUPS and s == 1:
                    jobs += [("load", u - GROUPS - 1), ("load_kb", u - GROUPS - 1), ("stage_v", u - GROUPS - 1)]
            n = u * TILES + s
            maxima = max_tiles(tiles_before(n, not tail_before), tiles_before(n + 1, not tail_before))
            if not project_next:
                maxima = [tile for tile in maxima if tile[0] < UNITS]
            any_before = tail_before or (u, s) != (0, 0)
            pv = divmod(u * TILES + s - 1, TILES) if any_before else None
            steps.append(Step((u, s), maxima, pv, u - 1 if s == 0 and any_before else None, jobs))
    if not project_next:
        steps.append(Step(None, [], (UNITS - 1, TILES - 1), UNITS - 1))
    return steps


def opening_steps():
    steps = [Step(jobs=[("weights", 0), ("x_load", 0)] + PROJECT_FIRST)]
    for step in range(OPENING_LEAD):
        chain = [("max_split", 0), ("warm", WHILE_SPLIT), ("max_rows", 0)] if step == TILES else []
        steps.append(Step(maxima=max_tiles(2 * step, 2 * step + 2), jobs=chain))
    steps[-1].jobs.append(("warm", WARMING))
    return steps


def closing_steps():
    steps = [Step(jobs=j) for _, j in sorted(tail_jobs(1).items())]
    at = [n for n, step in enumerate(steps) if ("x1T", 1) in step.jobs][0]
    return steps[:at] + [Step(jobs=[("warm", WHILE_NORM), ("x1T", 1), ("warm", KEEPING_WARM)])] + steps[at + 1:]


class Segment:

    def __init__(self, steps):
        self.steps = steps
        self.total = dict.fromkeys(NAMES, 0)
        self.number = {}
        for n, step in enumerate(steps):
            if step.exp:
                for hh in HEAD_ORDER:
                    self._count("score", ("exp", step.exp, hh))
            for tile in step.maxima:
                self._count("row", ("max", tile))
            if step.pv:
                self._count("pv", step.pv)
            if step.finished is not None:
                self._count("saved", step.finished)
            for job in step.jobs:
                for name, by in counts_of(job).items():
                    self._count(name, job, by)

    def _count(self, name, key, by=1):
        self.total[name] += by
        self.number[name, key] = self.total[name]

    def after(self, name, key):
        return self.base[name] + self.number.get((name, key), 0)


def build(nc, x, x_t, w, out):
    opening = Segment(opening_steps())
    first = Segment(batch_steps(True, False))
    middle = Segment(batch_steps(True, True))
    last = Segment(batch_steps(False, True))
    closing = Segment(closing_steps())
    loops = BATCH - 2

    def start_of(segment, i=0):
        before = {opening: [], first: [opening], middle: [opening, first], last: [opening, first] + [middle] * loops,
                  closing: [opening, first] + [middle] * loops + [last]}[segment]
        base = {n: sum(s.total[n] for s in before) for n in NAMES}
        if segment is middle:
            base = {n: i * middle.total[n] + base[n] if middle.total[n] else base[n] for n in NAMES}
        segment.base = base
        segment.opening, segment.closing = segment is opening, segment is closing
        segment.batch = {opening: -1, first: 0, middle: i + 1, last: BATCH - 1, closing: BATCH}[segment]

    def program(eng, emit):
        for segment in (opening, first):
            start_of(segment)
            emit(segment)
        with eng.Fori(0, loops) as i:
            start_of(middle, i)
            emit(middle)
        for segment in (last, closing):
            start_of(segment)
            emit(segment)

    def wait(eng, sem, count):
        if not isinstance(count, int) or count > 0:
            eng.wait_ge(sem, count)

    def last_of_group(i):
        return (GROUPS + i if i >= 0 else -1, TILES - 1)

    def alone(eng):
        eng.nop(nofuse=True)

    with ExitStack() as ctx:
        def sb(name, shape, dt):
            return ctx.enter_context(nc.sbuf_tensor(name, shape, dt))

        wt = sb("wt", [P, W_COLS], F32)
        zeros = sb("zeros", [P, HALF], BF16)
        first_exp = sb("first_exp", [P, 1], F32)
        ident_b = sb("ident_b", [P, P], BF16)
        w_ac = sb("w_ac", [P, 2 * CR], F32)
        b_ac = sb("b_ac", [P, 2], F32)
        wqs_s = sb("wqs_s", [P, P], F32)
        bqs_s = sb("bqs_s", [P, H], F32)
        bq_t = sb("bq_t", [P, 1], F32)
        xT = sb("xT", [P, TOK], F32)
        k3v = sb("k3v", [P, TOK], F32)
        cross = sb("cross", [P, TOK], F32)
        val = [sb("q_val", [P, TOK], F32), sb("k_val", [P, TOK], F32), sb("kb_val", [KB_ROWS, HALF], F32)]
        parts = [sb("q_parts", [P, 3, TOK], BF16), sb("k_parts", [P, 3, TOK], BF16), sb("kb_parts", [KB_ROWS, 3, HALF], BF16)]
        rest = sb("rest", [P, TOK], F32)
        v_next = sb("v_next", [P, TILES, D], F32)
        v_cur = sb("v_cur", [P, TILES, H, VW], F32)
        q_op = sb("q_op", [P, H // 2, TOK], BF16)
        k_op = sb("k_op", [P, H // 2, TOK], BF16)
        probs = sb("probs", [P, 2, GH, HALF], F32)
        neg_max = sb("neg_max", [P, 2, GH, HT], F32)
        max_parts = sb("max_parts", [P, GH, 3, HT], BF16)
        max_rest = sb("max_rest", [P, 2, GH, HT], F32)
        max_row = sb("max_row", [GH * 3 * HT, P], BF16)
        attn = sb("attn", [P, 2, GROUPS, HALF], F32)
        recip = sb("recip", [P, HT, H], F32)
        o_tok = sb("o_tok", [P, HT, D], F32)
        oT = sb("oT", [P, HALF], F32)
        resid_in = sb("resid_in", [P, HT, D], F32)
        resid_bo = sb("resid_bo", [P, HT, D], F32)
        pre_ln = sb("pre_ln", [P, HT, D], F32)
        stats = sb("stats", [P, HT, 6], F32)
        mean_var = sb("mean_var", [P, HT, 2], F32)
        rstd = sb("rstd", [P, HT], F32)
        minus_half = sb("minus_half", [P, HT], F32)
        x1 = sb("x1", [P, HT, D], F32)
        x1_b2 = sb("x1_b2", [P, HT, D], F32)
        x1T = sb("x1T", [P, HALF], F32)
        hid = sb("hid", [P, FC, HALF], F32)
        y = sb("y", [P, HT, D], F32)

        row_bank = [ctx.enter_context(nc.psum_tensor(f"row_bank{i}", [P, TOK], F32)) for i in range(ROW_RING)]
        score_bank = [ctx.enter_context(nc.psum_tensor(f"score_bank{i}", [P, HALF], F32)) for i in range(SCORE_RING)]
        pv_bank = ctx.enter_context(nc.psum_tensor("pv_bank", [P, HALF], F32))

        stacked = [nc.dram_tensor(f"stacked_{n}", (P, 6, TOK), BF16, kind="Internal").ap() for n in "qk"]
        stacked_kb = nc.dram_tensor("stacked_kb", (H, 3, TOK), BF16, kind="Internal").ap()
        stacked_max = nc.dram_tensor("stacked_max", (2, GH * 3 * HT, P), BF16, kind="Internal").ap()

        S = {n: ctx.enter_context(nc.semaphore(n)) for n in
             ("w_first", "w_rest", "zeros_ready", "cleared", "v_zeroed", "prepared", "score_filled", "score_read", "row_filled", "row_read",
              "pv_done", "attn_saved", "x_loaded", "parts_split", "group0_stored", "group1_stored",
              "group2_stored", "group3_stored", "kb_stored", "group0_loaded", "group1_loaded",
              "group2_loaded", "group3_loaded", "values_staged", "max_split", "max_stored", "shift0_loaded",
              "shift1_loaded", "resid_loaded", "resid_biased", "ln_stats", "rstd_ready", "ln1_done", "x1_biased", "out_ready", "out_stored",
              "dve_step", "pool_step")}
        group_stored = [S[f"group{g}_stored"] for g in range(GROUPS)]
        group_loaded = [S[f"group{g}_loaded"] for g in range(GROUPS)]
        shift_loaded = [S["shift0_loaded"], S["shift1_loaded"]]

        def W(name, a=0, n=None, rows=slice(0, P)):
            at, width = _W[name]
            return wt[rows, at + a:at + (width if n is None else a + n)]

        def col(name, i=0, rows=slice(0, P)):
            return W("cols", COL[name] + i, 1, rows)

        def half_of(t, h):
            return t[:, h * HALF:(h + 1) * HALF]

        def by_tile(bank):
            return bank.rearrange("p (t d) -> p t d", d=D)

        def head_rows(hh):
            return 64 * (hh % 2), hh // 2

        block = ctx.enter_context(nc.Block())

        @block.tensor
        def _(pe):
            def emit(seg):
                def score_slot(key):
                    n = seg.number["score", key] - 1
                    wait(pe, S["score_read"], seg.base["score"] + max(n - SCORE_RING + 1, 0))
                    return score_bank[n % SCORE_RING]

                def row_slot(key):
                    n = seg.number["row", key] - 1
                    wait(pe, S["row_read"], seg.base["row"] + max(n - ROW_RING + 1, 0))
                    return row_bank[n % ROW_RING]

                def scores(u, c, hh):
                    r, pair = head_rows(hh)
                    qh, g = divmod(u, GROUPS)
                    bank = score_slot(("exp", (u, c), hh))
                    rows = slice(r, r + KS)
                    nc.tensor.matmul(bank[:], k_op[rows, 2 * g + pair, c * P:(c + 1) * P],
                                     q_op[rows, 2 * g + pair, qh * HALF:(qh + 1) * HALF],
                                     start=True, stop=True).then_inc(S["score_filled"], 1)

                def max_pass(tiles):
                    for tile in tiles:
                        unit, t, hh = tile
                        r, pair = head_rows(hh)
                        qh, g = divmod(unit % UNITS, GROUPS)
                        if t == 0 and hh == 1:
                            wait(pe, group_loaded[g], seg.after(f"loaded{g}", ("load_kb", g)) if unit >= UNITS
                                 or unit < 2 else seg.after(f"loaded{g}", ("load_kb", g - GROUPS)))
                        bank = row_slot(("max", tile))
                        q0 = qh * HALF + t * P
                        for kh in range(2):
                            mm = nc.tensor.matmul(half_of(bank, kh), q_op[r:r + KB, 2 * g + pair, q0:q0 + P],
                                                  half_of(k_op[r:r + KB, 2 * g + pair], kh), start=True, stop=True)
                            if kh:
                                mm.then_inc(S["row_filled"], 1)
                            yield

                def values(u, c):
                    g = u % GROUPS
                    wait(pe, S["score_read"], seg.after("score", ("exp", (u, c), LAST_HEAD)))
                    if c == 0:
                        wait(pe, S["attn_saved"], seg.after("saved", u - 1))
                        if u < GROUPS:
                            wait(pe, S["values_staged"], seg.after("staged", ("stage_v", u - GROUPS)))
                    for hh in range(GH):
                        mm = nc.tensor.matmul(pv_bank[VW * hh:VW * (hh + 1), :], v_cur[:, c, GH * g + hh, :],
                                              probs[:, c % 2, hh, :], start=(c == 0), stop=(c == TILES - 1))
                    mm.then_inc(S["pv_done"], 1)

                def job(kind, i):
                    if kind == "weights":
                        pe.wait_ge(S["w_first"], 16)
                        bank = score_slot((kind, i))
                        for n, (a, s, b) in enumerate((("wk", "selAC", "bk"), ("wv", "selBD", "bv"))):
                            nc.tensor.matmul(bank[:, n * CR:(n + 1) * CR], W(a), W(s), start=True, stop=True)
                            mm = nc.tensor.matmul(bank[0:CR, 2 * CR + n:2 * CR + n + 1], W(s), col(b),
                                                  start=True, stop=True)
                        mm.then_inc(S["score_filled"], 1)
                    elif kind in ("q", "ac"):
                        wait(pe, S["x_loaded"], seg.after("x", ("x_load", 0)))
                        if kind == "ac" and seg.opening:
                            pe.wait_ge(S["score_read"], seg.after("score", ("weights", 0)))
                        bank = score_slot((kind, i))
                        lhs, rows = (W("wqT"), P) if kind == "q" else (w_ac[:, 0:CR], CR)
                        nc.tensor.matmul(bank[0:rows, :], lhs, half_of(xT, i), start=True,
                                         stop=True).then_inc(S["score_filled"], 1)
                    elif kind == "bd":
                        bank = row_slot((kind, i))
                        nc.tensor.matmul(bank[0:CR, 0:HALF], w_ac[:, CR:2 * CR], half_of(xT, i), start=True,
                                         stop=True).then_inc(S["row_filled"], 1)
                    elif kind == "k":
                        wait(pe, S["row_read"], seg.after("row", ("bd", i)))
                        if seg.opening and i == 0:
                            pe.wait_ge(S["prepared"], 6)
                        bank = score_slot((kind, i))
                        nc.tensor.matmul(bank[:], W("wkT"), half_of(xT, i), start=True, stop=False)
                        nc.tensor.matmul(bank[:], wqs_s[0:CR, :], half_of(cross[0:CR], i), start=False,
                                         stop=True).then_inc(S["score_filled"], 1)
                    elif kind == "kbias":
                        bank = score_slot((kind, i))
                        for half in range(2):
                            mm = nc.tensor.matmul(bank[KB_AT * half:KB_AT * half + H, :], bqs_s[0:CR, :],
                                                  half_of(cross[0:CR], half), start=True, stop=True)
                        mm.then_inc(S["score_filled"], 1)
                    elif kind == "v":
                        if seg.opening:
                            pe.wait_ge(S["w_rest"], 16)
                        bank = by_tile(row_slot((kind, i))[:])
                        for t in range(TILES):
                            mm = nc.tensor.matmul(bank[:, t, :], xT[:, t * P:(t + 1) * P], W("wvT"),
                                                  start=True, stop=True)
                        mm.then_inc(S["row_filled"], 1)
                    elif kind == "max_rows":
                        wait(pe, S["max_split"], seg.after("max_split", ("max_split", i)))
                        bank = score_slot((kind, i))[:].bitcast(BF16)
                        alone(pe)
                        nc.tensor.transpose(bank[0:GH * 3 * HT, 0:P], max_parts[:].rearrange("p h r t -> p (h r t)"),
                                            ident_b[:]).then_inc(S["score_filled"], 1)
                    elif kind == "norm":
                        half, t = i
                        wait(pe, S["attn_saved"], seg.after("saved", GROUPS - 1 if half == 0 else -1))
                        bank = by_tile(row_slot((kind, i))[:])
                        for g in range(GROUPS):
                            mm = nc.tensor.transpose(bank[:, g, :], attn[:, half, g, t * P:(t + 1) * P], W("ident"))
                        mm.then_inc(S["row_filled"], 1)
                    elif kind == "warm":
                        for _ in range(i):
                            nc.tensor.matmul(pv_bank[:], zeros[:, 0:P], zeros[:], start=True, stop=True)
                    elif kind == "oT":
                        wait(pe, S["row_read"], seg.after("row", ("norm", (i, HT - 1))))
                        bank = score_slot((kind, i))
                        for t in range(HT):
                            mm = nc.tensor.transpose(bank[:, t * P:(t + 1) * P], o_tok[:, t, :], W("ident"))
                        mm.then_inc(S["score_filled"], 1)
                    elif kind == "wo":
                        wait(pe, S["score_read"], seg.after("score", ("oT", i)))
                        bank = by_tile(row_slot((kind, i))[:])
                        for t in range(HT):
                            mm = nc.tensor.matmul(bank[:, t, :], oT[:, t * P:(t + 1) * P], W("woT"),
                                                  start=True, stop=True)
                        mm.then_inc(S["row_filled"], 1)
                    elif kind == "x1T":
                        wait(pe, S["ln1_done"], seg.after("ln1", ("stats1", i)))
                        bank = score_slot((kind, i))
                        for t in range(HT):
                            mm = nc.tensor.transpose(bank[:, t * P:(t + 1) * P], x1[:, t, :], W("ident"))
                        mm.then_inc(S["score_filled"], 1)
                    elif kind == "ffn1":
                        half, c = i
                        wait(pe, S["score_read"], seg.after("score", ("x1T", half)))
                        bank = score_slot((kind, i))
                        nc.tensor.matmul(bank[:], W("w1", c * P, P), x1T[:], start=True,
                                         stop=True).then_inc(S["score_filled"], 1)
                    elif kind == "ffn2":
                        half, part = i
                        wait(pe, S["score_read"], seg.after("score", ("ffn1", (half, FC - 1))))
                        bank = by_tile(row_slot((kind, i))[:])
                        for t in range(HT // 2 * part, HT // 2 * (part + 1)):
                            for c in range(FC):
                                mm = nc.tensor.matmul(bank[:, t, :], hid[:, c, t * P:(t + 1) * P], W("w2", c * P, P),
                                                      start=(c == 0), stop=(c == FC - 1))
                        mm.then_inc(S["row_filled"], 1)

                for step in seg.steps:
                    rows = max_pass(step.maxima)
                    if step.exp:
                        u, c = step.exp
                        if c == 0:
                            key = ("max_rows", u)
                            wait(pe, shift_loaded[u % 2], seg.after(f"shift{u % 2}", key))
                        for hh in HEAD_ORDER:
                            if hh == LAST_HEAD and not step.maxima and step.pv:
                                values(*step.pv)
                            scores(u, c, hh)
                            next(rows, None)
                    for _ in rows:
                        pass
                    if step.pv and (step.maxima or not step.exp):
                        values(*step.pv)
                    for kind, i in step.jobs:
                        job(kind, i)

            pe.wait_ge(S["zeros_ready"], 1)
            for _ in range(FIRST_WARMING):
                nc.tensor.matmul(pv_bank[:], zeros[:, 0:P], zeros[:], start=True, stop=True)
            program(pe, emit)

        @block.scalar
        def _(act):
            def emit(seg):
                def filled(key):
                    n = seg.number["score", key] - 1
                    wait(act, S["score_filled"], seg.base["score"] + n + 1)
                    return score_bank[n % SCORE_RING]

                def job(kind, i):
                    if kind == "weights":
                        bank = filled((kind, i))
                        nc.scalar.activation(w_ac[:], bank[:, 0:2 * CR], ACT.Identity)
                        nc.scalar.activation(b_ac[0:CR, 0:1], bank[0:CR, 2 * CR:2 * CR + 1], ACT.Identity,
                                             bias=col("bksAC", rows=slice(0, CR)))
                        nc.scalar.activation(b_ac[0:CR, 1:2], bank[0:CR, 2 * CR + 1:2 * CR + 2], ACT.Identity,
                                             bias=col("bvsBD", rows=slice(0, CR))).then_inc(S["score_read"], 1)
                    elif kind == "ac":
                        bank = filled((kind, i))
                        if seg.opening and i == 0:
                            act.wait_ge(S["score_read"], seg.after("score", ("weights", 0)))
                        nc.scalar.activation(half_of(k3v[0:CR], i), bank[0:CR, :], ACT.Identity,
                                             bias=b_ac[0:CR, 0:1]).then_inc(S["score_read"], 1)
                    elif kind in ("q", "k", "kbias"):
                        bank = filled((kind, i))
                        which = ("q", "k", "kbias").index(kind)
                        if i == 0:
                            wait(act, S["parts_split"], seg.base["split"])
                        if kind == "q":
                            if seg.opening and i == 0:
                                act.wait_ge(S["prepared"], 2)
                            nc.scalar.activation(half_of(val[0], i), bank[:], ACT.Identity, scale=col("temp"),
                                                 bias=bq_t[:]).then_inc(S["score_read"], 1)
                        elif kind == "k":
                            nc.scalar.activation(half_of(val[1], i), bank[:], ACT.Identity,
                                                 bias=col("bk")).then_inc(S["score_read"], 1)
                        else:
                            for half in range(2):
                                rows = slice(KB_AT * half, KB_AT * half + H)
                                last = nc.scalar.activation(val[2][rows], bank[rows, :], ACT.Identity)
                            last.then_inc(S["score_read"], 1)
                    elif kind == "max_rows":
                        bank = filled((kind, i))
                        wait(act, S["max_stored"], seg.after("max_stored", (kind, i)) - 16)
                        nc.scalar.activation(max_row[:], bank[:].bitcast(BF16)[0:GH * 3 * HT, 0:P],
                                             ACT.Identity).then_inc(S["score_read"], 1)
                    elif kind == "oT":
                        bank = filled((kind, i))
                        nc.scalar.activation(oT[:], bank[:], ACT.Identity).then_inc(S["score_read"], 1)
                    elif kind == "x1T":
                        bank = filled((kind, i))
                        nc.scalar.activation(x1T[:], bank[:], ACT.Identity).then_inc(S["score_read"], 1)
                    elif kind == "ffn1":
                        bank = filled((kind, i))
                        nc.scalar.activation(hid[:, i[1], :], bank[:], ACT.Relu,
                                             bias=col("b1", i[1])).then_inc(S["score_read"], 1)

                for step in seg.steps:
                    if step.exp:
                        u, c = step.exp
                        wait(act, S["pv_done"], seg.after("pv", divmod(TILES * u + c - 2, TILES)))
                        for hh in HEAD_ORDER:
                            bank = filled(("exp", (u, c), hh))
                            nc.scalar.activation(probs[:, c % 2, hh, :], bank[:], ACT.Exp).then_inc(S["score_read"], 1)
                    if step.finished is not None:
                        wait(act, S["pv_done"], seg.after("pv", step.pv))
                        qh, g = divmod(step.finished % UNITS, GROUPS)
                        nc.scalar.activation(attn[:, qh, g, :], pv_bank[:], ACT.Identity).then_inc(S["attn_saved"], 1)
                    for kind, i in step.jobs:
                        job(kind, i)

            act.wait_ge(S["zeros_ready"], 1)
            nc.scalar.activation(first_exp[:], zeros[:, 0:1], ACT.Exp)
            act.wait_ge(S["w_first"], 16)
            program(act, emit)

        @block.vector
        def _(dve):
            done = [0]

            def emit(seg):
                done[0] = 0

                def then(ins):
                    done[0] += 1
                    ins.then_inc(S["dve_step"], 1)
                    dve.wait_ge(S["dve_step"], seg.base["dve_step"] + done[0])

                def filled(key):
                    n = seg.number["row", key] - 1
                    wait(dve, S["row_filled"], seg.base["row"] + n + 1)
                    return row_bank[n % ROW_RING]

                def statistics(tiles):
                    for t in tiles:
                        last = nc.vector.bn_stats(stats[:, t, :], pre_ln[:, t, :])
                    return last

                def mean_and_variance(to, done_sem, left):
                    then(statistics(range(HT - left, HT)))
                    alone(dve)
                    for t in range(HT):
                        last = nc.vector.bn_aggr(mean_var[:, t, :], stats[:, t, :])
                    last.then_inc(S["ln_stats"], 1)
                    if seg.closing:
                        dve.wait_ge(S["rstd_ready"], 1 if to is x1 else 2)
                        if to is y:
                            dve.wait_ge(S["out_stored"], seg.base["out_stored"])
                        for t in range(HT):
                            last = nc.vector.tensor_scalar(to[:, t, :], pre_ln[:, t, :], mean_var[:, t, 0:1],
                                                           rstd[:, t:t + 1], ALU.subtract, ALU.mult)
                        last.then_inc(done_sem, 1)

                def job(kind, i):
                    if kind == "bd":
                        bank = filled((kind, i))
                        dve.wait_ge(S["score_read"], seg.after("score", ("ac", i)))
                        nc.vector.scalar_tensor_tensor(out=half_of(cross[0:CR], i), in0=bank[0:CR, 0:HALF],
                                                       scalar=b_ac[0:CR, 1:2], in1=half_of(k3v[0:CR], i),
                                                       op0=ALU.add, op1=ALU.mult).then_inc(S["row_read"], 1)
                    elif kind == "split_first":
                        which, half = i
                        rows = KB_ROWS if which == 2 else P
                        cols = slice(HALF * half, HALF * (half + 1))
                        v, part, r = val[which][:, cols], parts[which][:, :, cols], rest[0:rows, cols]
                        dve.wait_ge(S["score_read"], seg.after("score", (("q", "k", "kbias")[which], half)))
                        wait(dve, S["parts_split"], seg.after("split", (kind, i)) - 1)
                        then(nc.vector.tensor_copy(part[:, 0, :], v))
                        then(nc.vector.tensor_tensor(r, v, part[:, 0, :], ALU.subtract))
                        then(nc.vector.tensor_copy(part[:, 1, :], r))
                        nc.vector.tensor_tensor(part[:, 2, :], r, part[:, 1, :],
                                                ALU.subtract).then_inc(S["parts_split"], 1)
                    elif kind == "v":
                        bank = filled((kind, i))
                        wait(dve, S["values_staged"], seg.after("staged", ("stage_v", -1)))
                        bv = W("bv_row").unsqueeze(1).broadcast_to([P, TILES, D])
                        nc.vector.tensor_tensor(v_next[:], by_tile(bank[:]), bv, ALU.add).then_inc(S["row_read"], 1)
                    elif kind == "max_split":
                        buf = i % 2
                        tile = ("max", (i, HT - 1, GH - 2))
                        dve.wait_ge(S["row_read"], seg.after("row", tile))
                        nm, r = neg_max[:, buf], max_rest
                        then(nc.vector.tensor_copy(max_parts[:, :, 0, :], nm))
                        then(nc.vector.tensor_tensor(r[:, 0], nm, max_parts[:, :, 0, :], ALU.subtract))
                        then(nc.vector.tensor_copy(max_parts[:, :, 1, :], r[:, 0]))
                        nc.vector.tensor_tensor(max_parts[:, :, 2, :], r[:, 0], max_parts[:, :, 1, :],
                                                ALU.subtract).then_inc(S["max_split"], 1)
                    elif kind == "norm":
                        bank = filled((kind, i))
                        heads = bank[:, 0:GROUPS * P].rearrange("p (h r) -> p h r", r=VW)
                        then(nc.vector.reciprocal(recip[:, i[1], :], heads[:, :, HD]))
                        nc.vector.tensor_tensor(o_tok[:, i[1], :].rearrange("p (h d) -> p h d", d=HD),
                                                heads[:, :, 0:HD], recip[:, i[1], :].unsqueeze(2).broadcast_to([P, H, HD]),
                                                ALU.mult).then_inc(S["row_read"], 1)
                    elif kind == "wo":
                        bank = filled((kind, i))
                        wait(dve, S["resid_biased"], seg.after("resid_bo", ("resid", i)))
                        wait(dve, S["out_ready"], seg.after("out", ("stats2", i)) - 1)
                        b = by_tile(bank[:, 0:HALF])
                        nc.vector.tensor_tensor(pre_ln[:], b, resid_bo[:], ALU.add).then_inc(S["row_read"], 1)
                        dve.wait_ge(S["row_read"], seg.after("row", (kind, i)))
                        statistics(range(HT // 2))
                    elif kind == "ffn2":
                        bank = filled((kind, i))
                        half, part = i
                        wait(dve, S["x1_biased"], seg.after("x1_b2", ("stats1", half)))
                        tiles = slice(HT // 2 * part, HT // 2 * (part + 1))
                        nc.vector.tensor_tensor(pre_ln[:, tiles], by_tile(bank[:, 0:HALF])[:, tiles],
                                                x1_b2[:, tiles], ALU.add).then_inc(S["row_read"], 1)
                        dve.wait_ge(S["row_read"], seg.after("row", (kind, i)))
                        statistics(range(tiles.start, HT - 1 if part else tiles.stop))
                    elif kind == "stats1":
                        mean_and_variance(x1, S["ln1_done"], HT // 2)
                    elif kind == "stats2":
                        mean_and_variance(y, S["out_ready"], 1)

                for step in seg.steps:
                    for tile in step.maxima:
                        unit, t, hh = tile
                        bank = filled(("max", tile))
                        nc.vector.tensor_reduce(neg_max[:, unit % 2, hh, t:t + 1], bank[:], AX_X, ALU.max,
                                                negate=True).then_inc(S["row_read"], 1)
                    for kind, i in step.jobs:
                        job(kind, i)
                    
            nc.vector.memset(zeros[:].bitcast(F32), 0.0).then_inc(S["zeros_ready"], 1)
            nc.vector.memset(val[2][:], 0.0).then_inc(S["prepared"], 1)
            dve.wait_ge(S["w_first"], 16)
            nc.vector.tensor_scalar(bq_t[:], col("bq"), col("temp"), None, ALU.mult).then_inc(S["prepared"], 1)
            nc.vector.tensor_copy(ident_b[:], W("ident")).then_inc(S["prepared"], 1)
            nc.vector.memset(k_op[:].rearrange("p a t -> p (a t)").bitcast(F32), TWO_ONES).then_inc(S["cleared"], 1)
            dve.wait_ge(S["w_rest"], 16)
            nc.vector.tensor_scalar(wqs_s[0:CR], W("wqs", rows=slice(0, CR)), col("sign", rows=slice(0, CR)), None,
                                    ALU.mult).then_inc(S["prepared"], 1)
            nc.vector.tensor_scalar(bqs_s[0:CR], W("bqs", rows=slice(0, CR)), col("sign", rows=slice(0, CR)),
                                    col("temp", rows=slice(0, CR)), ALU.mult, ALU.mult).then_inc(S["prepared"], 1)
            nc.vector.memset(minus_half[:], -0.5).then_inc(S["prepared"], 1)
            program(dve, emit)

        @block.gpsimd
        def _(pool):
            def emit(seg):
                done = [0]

                def then(ins):
                    done[0] += 1
                    ins.then_inc(S["pool_step"], 1)
                    pool.wait_ge(S["pool_step"], seg.base["pool_step"] + done[0])
                    alone(pool)

                def normalise(to, key):
                    pool.wait_ge(S["ln_stats"], seg.after("ln_stats", key))
                    alone(pool)
                    then(nc.gpsimd.tensor_scalar(rstd[:], mean_var[:, :, 1], EPS, None, ALU.add))
                    power = nc.gpsimd.tensor_tensor(rstd[:], rstd[:], minus_half[:], ALU.pow)
                    if seg.closing:
                        power.then_inc(S["rstd_ready"], 1)
                        return None
                    then(power)
                    for t in range(HT):
                        last = nc.gpsimd.tensor_scalar(to[:, t, :], pre_ln[:, t, :], mean_var[:, t, 0:1],
                                                       rstd[:, t:t + 1], ALU.subtract, ALU.mult)
                    return last

                def job(kind, i):
                    if kind == "split":
                        rows = KB_ROWS if i == 2 else P
                        v, part, r = val[i], parts[i], rest[0:rows, 0:HALF if i == 2 else TOK]
                        pool.wait_ge(S["score_read"], seg.after("score", (("q", 1), ("k", 1), ("kbias", 0))[i]))
                        alone(pool)
                        for g in range(GROUPS):
                            wait(pool, group_stored[g], seg.base[f"stored{g}"])
                            alone(pool)
                        wait(pool, S["kb_stored"], seg.base["kb_stored"])
                        alone(pool)
                        then(nc.gpsimd.tensor_copy(part[0:rows, 0, :], v[:]))
                        then(nc.gpsimd.tensor_tensor(r, v[:], part[0:rows, 0, :], ALU.subtract))
                        then(nc.gpsimd.tensor_copy(part[0:rows, 1, :], r))
                        nc.gpsimd.tensor_tensor(part[0:rows, 2, :], r, part[0:rows, 1, :],
                                                ALU.subtract).then_inc(S["parts_split"], 1)
                    elif kind == "stage_v":
                        pool.wait_ge(S["row_read"], seg.after("row", ("v", min(i, 0))))
                        if not seg.opening:
                            pool.wait_ge(S["pv_done"], seg.after("pv", last_of_group(i)))
                        alone(pool)
                        g = i % GROUPS
                        heads = slice(GH * g, GH * (g + 1))
                        nc.gpsimd.tensor_copy(v_cur[:, :, heads, 0:HD],
                                              v_next[:].rearrange("p t (h d) -> p t h d", d=HD)[:, :, heads, :])\
                            .then_inc(S["values_staged"], 1)
                    elif kind == "resid":
                        wait(pool, S["resid_loaded"], seg.after("resid", (kind, i)))
                        wait(pool, S["ln1_done"], seg.after("ln1", ("stats1", i)) - 1)
                        nc.gpsimd.tensor_tensor(resid_bo[:], resid_in[:],
                                                W("bo_row").unsqueeze(1).broadcast_to([P, HT, D]),
                                                ALU.add).then_inc(S["resid_biased"], 1)
                    elif kind == "stats1":
                        last = normalise(x1, (kind, i))
                        if last:
                            last.then_inc(S["ln1_done"], 1)
                        pool.wait_ge(S["ln1_done"], seg.after("ln1", (kind, i)))
                        nc.gpsimd.tensor_tensor(x1_b2[:], x1[:], W("b2_row").unsqueeze(1).broadcast_to([P, HT, D]),
                                                ALU.add).then_inc(S["x1_biased"], 1)
                    elif kind == "stats2":
                        wait(pool, S["out_stored"], seg.after("out_stored", (kind, i)) - 16)
                        last = normalise(y, (kind, i))
                        if last:
                            last.then_inc(S["out_ready"], 1)

                for step in seg.steps:
                    for kind, i in step.jobs:
                        job(kind, i)

            nc.gpsimd.memset(q_op[:].rearrange("p a t -> p (a t)").bitcast(F32), TWO_ONES).then_inc(S["cleared"], 1)
            nc.gpsimd.memset(v_cur[:].rearrange("p c h w -> p (c h w)"), 0.0).then_inc(S["v_zeroed"], 1)
            pool.wait_ge(S["v_zeroed"], 1)
            nc.gpsimd.memset(v_cur[:].rearrange("p c h w -> p (c h) w")[:, :, HD:HD + 1], 1.0).then_inc(S["cleared"], 1)
            pool.wait_ge(S["w_rest"], 16)
            pool.wait_ge(S["cleared"], 3)
            pool.wait_ge(S["prepared"], 6)
            program(pool, emit)

        @block.sync
        def _(sp):
            def batch_rows(t, b, half=None):
                rows = t[bass.ds(b, 1)].rearrange("b (t p) d -> p (b t) d", p=P)
                return rows if half is None else rows[:, half * HT:(half + 1) * HT, :]

            def emit(seg):
                def job(kind, i):
                    if kind == "x_load":
                        if seg.opening:
                            return
                        sp.wait_ge(S["score_filled"], seg.base["score"])
                        alone(sp)
                        sp.wait_ge(S["row_filled"], seg.base["row"])
                        alone(sp)
                        sp.dma_start(xT[:].unsqueeze(1), x_t[bass.ds(seg.batch + 1, 1)].rearrange("b d t -> d b t"))\
                            .then_inc(S["x_loaded"], 16)
                    elif kind == "store":
                        wait(sp, group_loaded[i], seg.after(f"loaded{i}", ("load_kb", i - GROUPS)))
                        alone(sp)
                        rows = slice(GH * HD * i, GH * HD * (i + 1))
                        for op in range(2):
                            split = ("split_first", (op, 1)) if seg.opening else ("split", op)
                            sp.wait_ge(S["parts_split"], seg.after("split", split))
                            alone(sp)
                            for n, slots in ((0, slice(0, 3)), (1, slice(3, 5)), (2, slice(5, 6))):
                                width = slots.stop - slots.start
                                if op == 0:
                                    part = parts[0][rows, n, :].unsqueeze(1).broadcast_to([GH * HD, width, TOK])
                                else:
                                    part = parts[1][rows, 0:width, :]
                                sp.dma_start(stacked[op][rows, slots, :], part).then_inc(group_stored[i], 16)
                    elif kind == "store_kb":
                        sp.wait_ge(S["parts_split"], seg.after("split", ("split_first", (2, 0)) if seg.opening
                                                               else ("split", 2)))
                        alone(sp)
                        for g in range(GROUPS):
                            wait(sp, group_loaded[g], seg.after(f"loaded{g}", ("load_kb", g - GROUPS)))
                            alone(sp)
                        for half in range(2):
                            sp.dma_start(stacked_kb[:, :, half * HALF:(half + 1) * HALF],
                                         parts[2][KB_AT * half:KB_AT * half + H]).then_inc(S["kb_stored"], 16)
                    elif kind == "load":
                        g = i % GROUPS
                        sp.wait_ge(group_stored[g], seg.after(f"stored{g}", ("store", i)))
                        alone(sp)
                        if not seg.opening:
                            sp.wait_ge(S["pv_done"], seg.after("pv", last_of_group(i)))
                        for j in range(2):
                            heads = slice(GH * g + j, GH * (g + 1), 2)
                            pairs = slice(2 * g, 2 * g + 2)
                            for op, src in ((q_op, stacked[0]), (k_op, stacked[1])):
                                by_head = src.rearrange("(h d) s t -> h (d s) t", d=HD)
                                sp.dma_start(op[64 * j:64 * j + KM, pairs, :],
                                             by_head[heads].rearrange("h r t -> r h t"))\
                                    .then_inc(group_loaded[g], 16)
                    elif kind == "load_kb":
                        sp.wait_ge(S["kb_stored"], seg.after("kb_stored", ("store_kb", min(i, 0))))
                        alone(sp)
                        g = i % GROUPS
                        for j in range(2):
                            heads = slice(GH * g + j, GH * (g + 1), 2)
                            sp.dma_start(k_op[64 * j + KM:64 * j + KB, 2 * g:2 * g + 2, :],
                                         stacked_kb[heads].rearrange("h r t -> r h t")).then_inc(group_loaded[g], 16)
                    elif kind == "max_rows":
                        sp.wait_ge(S["score_read"], seg.after("score", (kind, i)))
                        sp.dma_start(stacked_max[i % 2], max_row[:]).then_inc(S["max_stored"], 16)
                        sp.wait_ge(S["max_stored"], seg.after("max_stored", (kind, i)))
                        qh, g = divmod(i % UNITS, GROUPS)
                        by_row = stacked_max[i % 2].rearrange("(a j r t) q -> a j r (t q)", a=2, j=2, r=3)
                        for j in range(2):
                            sp.dma_start(q_op[64 * j + KB:64 * j + KS, 2 * g:2 * g + 2, qh * HALF:(qh + 1) * HALF],
                                         by_row[:, j].rearrange("a r q -> r a q")).then_inc(shift_loaded[i % 2], 16)
                    elif kind == "resid":
                        wait(sp, S["resid_biased"], seg.after("resid_bo", (kind, i)) - 1)
                        alone(sp)
                        b = seg.batch - 1 if i == 1 else seg.batch
                        sp.dma_start(resid_in[:], batch_rows(x, b, i)).then_inc(S["resid_loaded"], 16)
                    elif kind == "stats2":
                        sp.wait_ge(S["out_ready"], seg.after("out", (kind, i)))
                        alone(sp)
                        b = seg.batch - 1 if i == 1 else seg.batch
                        sp.dma_start(batch_rows(out, b, i), y[:]).then_inc(S["out_stored"], 16)

                for step in seg.steps:
                    for kind, i in step.jobs:
                        job(kind, i)

            sp.dma_start(wt[:, 0:W_FIRST], w[:, 0:W_FIRST]).then_inc(S["w_first"], 16)
            sp.dma_start(xT[:], x_t[0]).then_inc(S["x_loaded"], 16)
            sp.dma_start(wt[:, W_FIRST:], w[:, W_FIRST:]).then_inc(S["w_rest"], 16)
            sp.wait_ge(S["cleared"], 3)
            program(sp, emit)
            sp.wait_ge(S["out_stored"], closing.after("out_stored", ("stats2", 1)))


def pack(i):
    f = np.float32
    Wks, Wvs, Wqs = (np.asarray(i["L0_attn_" + n], f) for n in ("Wks", "Wvs", "Wqs"))
    bks, bvs, bqs = (np.asarray(i["L0_attn_" + n], f) for n in ("bks", "bvs", "bqs"))
    get = lambda n: np.asarray(i["L0_attn_" + n], f)
    w = np.zeros((P, W_COLS), f)

    def put(name, a, at=0):
        a = np.atleast_2d(a)
        w[0:a.shape[0], _W[name][0] + at:_W[name][0] + at + a.shape[1]] = a

    put("ident", np.eye(P, dtype=f))
    put("wqT", get("Wq").T), put("wkT", get("Wk").T), put("wvT", get("Wv").T), put("woT", get("Wo").T)
    put("wk", get("Wk")), put("wv", get("Wv"))
    for h in range(H):
        for c in range(3):
            for at, kc, vc in ((0, (c + 1) % 3, (c + 2) % 3), (64, (c + 2) % 3, (c + 1) % 3)):
                r = at + 3 * h + c
                w[HD * h:HD * (h + 1), _W["selAC"][0] + r] = Wks[kc]
                w[HD * h:HD * (h + 1), _W["selBD"][0] + r] = Wvs[vc]
                w[r, _W["cols"][0] + COL["bksAC"]] = bks[kc]
                w[r, _W["cols"][0] + COL["bvsBD"]] = bvs[vc]
                w[r, _W["wqs"][0] + HD * h:_W["wqs"][0] + HD * (h + 1)] = Wqs[c]
                w[r, _W["bqs"][0] + h] = bqs[c]
    for name in ("bq", "bk", "bv"):
        put("cols", get(name)[:, None], COL[name])
    put("cols", np.full((P, 1), get("temp"), f), COL["temp"])
    put("cols", np.where(np.arange(P) < 64, 1, -1).astype(f)[:, None], COL["sign"])
    put("cols", np.asarray(i["L0_ffn_b1"], f).reshape(FC, P).T, COL["b1"])
    for name, b in (("bv_row", get("bv")), ("bo_row", get("bo")), ("b2_row", np.asarray(i["L0_ffn_b2"], f))):
        put(name, np.broadcast_to(b, (P, D)))
    put("w1", np.asarray(i["L0_ffn_W1"], f))
    put("w2", np.asarray(i["L0_ffn_W2"], f).reshape(FC, P, D).transpose(1, 0, 2).reshape(P, FC * D))
    return w


def kernel(**inputs):
    import concourse.bacc as bacc
    from concourse.bass_utils import run_bass_kernel_spmd

    nc = bacc.Bacc("TRN2", target_bir_lowering=False, num_devices=1)
    x_in = np.ascontiguousarray(inputs["L0_attn_x"])
    arrays = {"x": x_in, "x_t": np.ascontiguousarray(x_in.transpose(0, 2, 1)), "weights": pack(inputs)}
    x, x_t, w = (nc.dram_tensor(n, a.shape, F32, kind="ExternalInput").ap() for n, a in arrays.items())
    out = nc.dram_tensor("out", (BATCH, TOK, D), F32, kind="ExternalOutput").ap()
    build(nc, x, x_t, w, out)
    return run_bass_kernel_spmd(nc, [arrays], core_ids=[0]).results[0]["out"]
```
